# Optimizing a Trainium2 kernel written in Bass

```python
import numpy as np
import jax
import jax.numpy as jnp

def _softmax(x, axis=-1):
    return jax.nn.softmax(x, axis=axis)

def _gelu(x):
    return jax.nn.gelu(x, approximate=True)

def _silu(x):
    return jax.nn.silu(x)

def _sigmoid(x):
    return jax.nn.sigmoid(x)

def _layernorm(x, axis=-1, eps=1e-05):
    m = jnp.mean(x, axis=axis, keepdims=True)
    v = jnp.var(x, axis=axis, keepdims=True)
    return (x - m) / jnp.sqrt(v + eps)

def _scatter_add(tgt, idx, src, axis=0):
    return tgt.at[idx].add(src)

def _segment_sum(src, seg, n):
    return jax.ops.segment_sum(src, seg, n)
kernel_name = 'mk_prb_d1_jaxref_r8_8a7146'

def setup_inputs(seed: int=0):
    np.random.seed(seed)
    _w = jnp.asarray

    def _L0_attn_setup():
        import math
        import jax, jax.numpy as jnp
        import numpy as np
        N_HEAD = 16

        def _rope_cos_sin(l, head_dim):
            scale = jnp.arange(0, head_dim, 2, dtype=jnp.float32)[:head_dim // 2]
            freqs = 1.0 / 10000.0 ** scale
            angles = jnp.arange(l, dtype=jnp.float32)[:, None] * freqs[None, :]
            return (jnp.cos(angles), jnp.sin(angles))

        def _rope_apply(x, cos, sin):
            b, l, h, hd = x.shape
            xp = x.astype(jnp.float32).reshape(b, l, h, hd // 2, 2)
            xr, xi = (xp[..., 0], xp[..., 1])
            c = cos[None, :, None, :]
            s = sin[None, :, None, :]
            out_r = xr * c - xi * s
            out_i = xr * s + xi * c
            out = jnp.stack([out_r, out_i], axis=-1).reshape(b, l, h, hd)
            return out.astype(x.dtype)
        key = jax.random.key(seed)
        ks = jax.random.split(key, 9)
        b, l, d = (2, 256, 128)
        sc = 1.0 / math.sqrt(d)
        inp = {'x': jax.random.normal(ks[0], (b, l, d), dtype=jnp.float32), 'Wq': jax.random.normal(ks[1], (d, d), dtype=jnp.float32) * sc, 'bq': jnp.zeros((d,), dtype=jnp.float32), 'Wk': jax.random.normal(ks[2], (d, d), dtype=jnp.float32) * sc, 'bk': jnp.zeros((d,), dtype=jnp.float32), 'Wv': jax.random.normal(ks[3], (d, d), dtype=jnp.float32) * sc, 'bv': jnp.zeros((d,), dtype=jnp.float32), 'Wo': jax.random.normal(ks[4], (d, d), dtype=jnp.float32) * sc, 'bo': jnp.zeros((d,), dtype=jnp.float32)}
        return inp
    _L0_attn_in = _L0_attn_setup()

    def _L0_ffn_setup():
        import jax, jax.numpy as jnp
        import numpy as np
        DIM = 128
        HIDDEN = 384
        SCALE = 1.0 / 127.0

        def _dequant(w_int, dtype):
            return w_int.astype(dtype) * jnp.asarray(SCALE, dtype)
        key = jax.random.key(seed)
        k_x, k_g, k_u, k_d = jax.random.split(key, 4)
        x = jax.random.normal(k_x, (4, 256, DIM), dtype=jnp.float32)
        w_gate = jax.random.randint(k_g, (HIDDEN, DIM), -127, 128, dtype=jnp.int32)
        w_up = jax.random.randint(k_u, (HIDDEN, DIM), -127, 128, dtype=jnp.int32)
        w_down = jax.random.randint(k_d, (DIM, HIDDEN), -127, 128, dtype=jnp.int32)
        return {'x': x, 'w_gate': w_gate, 'w_up': w_up, 'w_down': w_down}
    _L0_ffn_in = _L0_ffn_setup()
    _d = {'L0_attn_x': _L0_attn_in['x'], 'L0_attn_Wq': _L0_attn_in['Wq'], 'L0_attn_bq': _L0_attn_in['bq'], 'L0_attn_Wk': _L0_attn_in['Wk'], 'L0_attn_bk': _L0_attn_in['bk'], 'L0_attn_Wv': _L0_attn_in['Wv'], 'L0_attn_bv': _L0_attn_in['bv'], 'L0_attn_Wo': _L0_attn_in['Wo'], 'L0_attn_bo': _L0_attn_in['bo'], 'L0_ffn_w_gate': _L0_ffn_in['w_gate'], 'L0_ffn_w_up': _L0_ffn_in['w_up'], 'L0_ffn_w_down': _L0_ffn_in['w_down']}
    _x0 = _d['L0_attn_x']
    _d['L0_attn_x'] = jax.random.normal(jax.random.fold_in(jax.random.key(seed), 1), (8, 256, 128), dtype=_x0.dtype)
    del _x0
    return _d

def reference(L0_attn_x, L0_attn_Wq, L0_attn_bq, L0_attn_Wk, L0_attn_bk, L0_attn_Wv, L0_attn_bv, L0_attn_Wo, L0_attn_bo, L0_ffn_w_gate, L0_ffn_w_up, L0_ffn_w_down):

    def _L0_attn_ref(x, Wq, bq, Wk, bk, Wv, bv, Wo, bo):
        import math
        import jax, jax.numpy as jnp
        import numpy as np
        N_HEAD = 16

        def _rope_cos_sin(l, head_dim):
            scale = jnp.arange(0, head_dim, 2, dtype=jnp.float32)[:head_dim // 2]
            freqs = 1.0 / 10000.0 ** scale
            angles = jnp.arange(l, dtype=jnp.float32)[:, None] * freqs[None, :]
            return (jnp.cos(angles), jnp.sin(angles))

        def _rope_apply(x, cos, sin):
            b, l, h, hd = x.shape
            xp = x.astype(jnp.float32).reshape(b, l, h, hd // 2, 2)
            xr, xi = (xp[..., 0], xp[..., 1])
            c = cos[None, :, None, :]
            s = sin[None, :, None, :]
            out_r = xr * c - xi * s
            out_i = xr * s + xi * c
            out = jnp.stack([out_r, out_i], axis=-1).reshape(b, l, h, hd)
            return out.astype(x.dtype)
        b, l, d = x.shape
        h = N_HEAD
        hd = d // h
        q = (x @ Wq + bq).reshape(b, l, h, hd)
        k = (x @ Wk + bk).reshape(b, l, h, hd)
        v = (x @ Wv + bv).reshape(b, l, h, hd)
        cos, sin = _rope_cos_sin(l, hd)
        q = _rope_apply(q, cos, sin)
        k = _rope_apply(k, cos, sin)
        score = jnp.einsum('blhd,bmhd->bhlm', q, k) / math.sqrt(hd)
        ctx = jnp.einsum('bhlm,bmhd->blhd', score, v).reshape(b, l, d)
        return ctx @ Wo + bo

    def _L0_ffn_ref(x, w_gate, w_up, w_down):
        import jax, jax.numpy as jnp
        import numpy as np
        DIM = 128
        HIDDEN = 384
        SCALE = 1.0 / 127.0

        def _dequant(w_int, dtype):
            return w_int.astype(dtype) * jnp.asarray(SCALE, dtype)
        wg = _dequant(w_gate, x.dtype)
        wu = _dequant(w_up, x.dtype)
        wd = _dequant(w_down, x.dtype)
        gate = jnp.einsum('bsd,hd->bsh', x, wg)
        up = jnp.einsum('bsd,hd->bsh', x, wu)
        h = jax.nn.silu(gate) * up
        return jnp.einsum('bsh,dh->bsd', h, wd)
    x = L0_attn_x
    xn = _layernorm(x, axis=-1)
    x = x + _L0_attn_ref(xn, L0_attn_Wq, L0_attn_bq, L0_attn_Wk, L0_attn_bk, L0_attn_Wv, L0_attn_bv, L0_attn_Wo, L0_attn_bo) + _L0_ffn_ref(xn, L0_ffn_w_gate, L0_ffn_w_up, L0_ffn_w_down)
    return x

_drawn_inputs = setup_inputs


def setup_inputs(seed=0):
    import zlib

    import numpy as np

    out = dict(_drawn_inputs(seed))
    spreads = {'L0_attn_bq': (0.0, 0.8),
     'L0_attn_bk': (0.0, 0.8),
     'L0_attn_bv': (0.0, 0.8),
     'L0_attn_bo': (0.0, 0.8)}
    factors = {}
    for name, (base, spread) in spreads.items():
        noise = np.random.default_rng([zlib.crc32(name.encode()), seed]).standard_normal(out[name].shape)
        drawn = base * np.exp(spread * noise) if base else spread * noise
        out[name] = jnp.asarray(drawn.astype(out[name].dtype))
    for name, factor in factors.items():
        out[name] = (out[name] * factor).astype(out[name].dtype)
    return out
```

```python
import concourse.bass as bass
from concourse import mybir
from contextlib import ExitStack

P = 128
B, L, D = 8, 256, 128
HEADS, HD = 16, 8
PAIRS = HD // 2
HIDDEN = 384
HB = HIDDEN // P
BPC = 2
CHUNKS = B // BPC
HALVES = L // P
TILES = BPC * HALVES
N = TILES * P
SWAP = D // 2
SCALE = 1.0 / 127.0
EPS = 1e-5


def build(nc, x, w_qkv, w_o, b_q, b_kv, b_o, w_ffn, tab_k, tab_q, head_mask, identity, out):
    f32, f32r, i32 = mybir.dt.float32, mybir.dt.float32r, mybir.dt.int32
    ALU = mybir.AluOpType
    ACT = mybir.ActivationFunctionType

    ctx = ExitStack()
    with ctx:
        def sb(name, shape, dt=f32):
            return ctx.enter_context(nc.sbuf_tensor(name, shape, dt))

        def pb(name):
            return ctx.enter_context(nc.psum_tensor(name, [P, N], f32))

        def sem(name):
            return ctx.enter_context(nc.semaphore(name))

        ident = sb("ident", [P, P])
        mask = sb("mask", [P, D])
        rope_k = sb("rope_k", [P, 2, HALVES, D])
        rope_q = sb("rope_q", [P, 2, L])
        wqkv = sb("wqkv", [P, 3 * D])
        wqkv_hi = sb("wqkv_hi", [P, 3 * D], f32r)
        wqkv_lo = sb("wqkv_lo", [P, 3 * D], f32r)
        wo = sb("wo", [P, D])
        bq = sb("bq", [P, 1])
        bo = sb("bo", [P, D])
        bkv = sb("bkv", [P, 2 * D])
        bkv_parts = sb("bkv_parts", [P, 2 * D], f32r)
        ones = sb("ones", [P, P], f32r)
        wf = sb("wf", [P, 3, HIDDEN], i32)
        wf_hi = sb("wf_hi", [P, 3, HIDDEN], f32r)
        wf_lo = sb("wf_lo", [P, 3, HIDDEN], f32r)
        xs = sb("xs", [P, CHUNKS, TILES, D])
        xres = sb("xres", [P, CHUNKS, TILES, D])
        xn = sb("xn", [P, CHUNKS, TILES, D])
        outs = sb("outs", [P, CHUNKS, TILES * D])
        bn = sb("bn", [P, CHUNKS, TILES, 6])
        mv = sb("mv", [P, CHUNKS, TILES, 2])
        minus_half = sb("minus_half", [P, TILES])
        veps = sb("veps", [P, CHUNKS, TILES])
        rstd = sb("rstd", [P, CHUNKS, TILES])
        neg_mean = sb("neg_mean", [P, CHUNKS, TILES])
        shift = sb("shift", [P, CHUNKS, TILES])
        xT_hi = sb("xT_hi", [P, 2, N], f32r)
        xT_lo = sb("xT_lo", [P, 2, N], f32r)
        q_cos = sb("q_cos", [P, 2, N])
        q_sin = sb("q_sin", [P, 2, N])
        k_cos = sb("k_cos", [P, 2, TILES, D])
        k_sin = sb("k_sin", [P, 2, TILES, D])
        k_rot = sb("k_rot", [P, 2, TILES, D])
        v = sb("v", [P, 2, TILES, D])
        kv = sb("kv", [P, BPC, D])
        kvo = sb("kvo", [P, BPC, D])
        kvo_swap = sb("kvo_swap", [P, BPC, D])
        silu = sb("silu", [P, 2, N])
        h = sb("h", [P, 2, N])
        h_hi = sb("h_hi", [P, 2, HB, N], f32r)
        h_lo = sb("h_lo", [P, 2, HB, N], f32r)

        p_gate = [pb("p_gate0"), pb("p_gate1")]
        p_up = [pb("p_up0"), pb("p_up1")]
        p_x = pb("p_x")
        p_kv = [pb("p_kv0"), pb("p_kv1")]
        p_out = pb("p_out")

        def out_bank(c, b):
            return p_x if c == CHUNKS - 1 and b == 1 else p_out

        x_in = [sem(f"x_in{c}") for c in range(CHUNKS)]
        ident_in, wqkv_in, wo_in, bq_in, bkv_in, bo_in, wf_in, tabk_in, tabq_in, mask_in = (
            sem(n) for n in ("ident_in", "wqkv_in", "wo_in", "bq_in", "bkv_in", "bo_in", "wf_in",
                             "tabk_in", "tabq_in", "mask_in"))
        out_done = sem("out_done")
        consts_set = sem("consts_set")
        bkv_zeroed = sem("bkv_zeroed")
        bkv_hi_done = sem("bkv_hi_done")
        bkv_ready = sem("bkv_ready")
        wqkv_hi_done = sem("wqkv_hi_done")
        wqkv_lo_done = sem("wqkv_lo_done")
        wf_hi_done = sem("wf_hi_done")
        wf_lo_done = sem("wf_lo_done")
        bn_done = sem("bn_done")
        mv_done = sem("mv_done")
        veps_done = sem("veps_done")
        rstd_done = sem("rstd_done")
        shift_done = sem("shift_done")
        xn_done = sem("xn_done")
        xres_done = sem("xres_done")
        xT_made = sem("xT_made")
        xT_hi_done = sem("xT_hi_done")
        xT_lo_done = sem("xT_lo_done")
        q_made = sem("q_made")
        q_rotated = sem("q_rotated")
        kv_made = sem("kv_made")
        v_done = sem("v_done")
        k_parts_done = sem("k_parts_done")
        k_rotated = sem("k_rotated")
        prod_made = sem("prod_made")
        prod_masked = sem("prod_masked")
        kvo_made = sem("kvo_made")
        kvo_done = sem("kvo_done")
        gu_made = sem("gu_made")
        silu_done = sem("silu_done")
        h_done = sem("h_done")
        h_hi_done = sem("h_hi_done")
        h_lo_done = sem("h_lo_done")
        out_made = sem("out_made")
        out_added = sem("out_added")

        block = ctx.enter_context(nc.Block())

        x_view = x.rearrange("(c b) (p h) d -> c p b (h d)", b=BPC, h=HALVES)
        out_view = out.rearrange("(c b) (p h) d -> c p b (h d)", b=BPC, h=HALVES)

        @block.sync
        def _(sp):
            def load_x(c):
                sp.dma_start(xs[:, c].rearrange("p (b h) d -> p b (h d)", b=BPC), x_view[c]).then_inc(x_in[c], 16)

            load_x(0)
            sp.dma_start(wqkv[:], w_qkv).then_inc(wqkv_in, 16)
            sp.dma_start(wf[:], w_ffn).then_inc(wf_in, 16)
            load_x(1)
            sp.dma_start(rope_q[:], tab_q).then_inc(tabq_in, 16)
            load_x(2)
            load_x(3)
            for c in range(CHUNKS):
                halves = 2 if c == CHUNKS - 1 else 1
                for s in range(halves):
                    sp.wait_ge(out_added, c + s + 1)
                    nb = BPC // halves
                    sp.dma_start(out_view[c][:, s * nb:(s + 1) * nb],
                                 outs[:, c].rearrange("p (b m) -> p b m", b=BPC)[:, s * nb:(s + 1) * nb]
                                 ).then_inc(out_done, 16)
            sp.wait_ge(out_done, 16 * (CHUNKS + 1))

        @block.gpsimd
        def _(pool):
            nc.gpsimd.memset(bkv[:], 0.0).then_inc(bkv_zeroed, 1)
            nc.gpsimd.memset(minus_half[:], -0.5).then_inc(consts_set, 1)
            nc.gpsimd.memset(ones[:].bitcast(f32), 1.0).then_inc(consts_set, 1)
            nc.gpsimd.memset(bkv_parts[:].bitcast(f32), 0.0).then_inc(consts_set, 1)

            def spread(c):
                pool.wait_ge(mv_done, TILES * (c + 1))
                nc.gpsimd.tensor_scalar(veps[:, c], mv[:, c, :, 1], EPS, None, ALU.add).then_inc(veps_done, 1)
                nc.gpsimd.tensor_scalar(neg_mean[:, c], mv[:, c, :, 0], -1.0, None, ALU.mult).then_inc(veps_done, 1)
                pool.wait_ge(veps_done, 2 * c + 2)
                if c == 0:
                    pool.wait_ge(consts_set, 1)
                nc.gpsimd.tensor_tensor(rstd[:, c], veps[:, c], minus_half[:], ALU.pow).then_inc(rstd_done, 1)
                pool.wait_ge(rstd_done, c + 1)
                nc.gpsimd.tensor_tensor(shift[:, c], neg_mean[:, c], rstd[:, c], ALU.mult).then_inc(shift_done, 1)

            def residual(c):
                if c == 0:
                    pool.wait_ge(bo_in, 16)
                pool.wait_ge(x_in[c], 16)
                nc.gpsimd.tensor_tensor(xres[:, c], xs[:, c],
                                        bo[:].rearrange("p (o d) -> p o d", o=1).to_broadcast([P, TILES, D]),
                                        ALU.add).then_inc(xres_done, 1)

            def rotate_k(c, b):
                pool.wait_ge(k_parts_done, 2 * (BPC * c + b + 1))
                t = slice(HALVES * b, HALVES * (b + 1))
                nc.gpsimd.tensor_tensor(k_rot[:, c % 2, t], k_cos[:, c % 2, t], k_sin[:, c % 2, t],
                                        ALU.add).then_inc(k_rotated, 1)

            def low_h(c, j):
                g = HB * c + j
                pool.wait_ge(h_hi_done, g + 1)
                nc.gpsimd.tensor_tensor(h_lo[:, c % 2, j], h[:, g % 2], h_hi[:, c % 2, j].bitcast(f32),
                                        ALU.subtract).then_inc(h_lo_done, 1)

            spread(0)
            spread(1)
            rotate_k(0, 0)
            rotate_k(0, 1)
            for c in range(CHUNKS):
                low_h(c, 0)
                if c + 2 < CHUNKS:
                    spread(c + 2)
                low_h(c, 1)
                residual(c)
                low_h(c, 2)
                if c + 1 < CHUNKS:
                    rotate_k(c + 1, 0)
                    rotate_k(c + 1, 1)

        @block.scalar
        def _(act):
            act.dma_start(ident[:], identity).then_inc(ident_in, 16)
            act.dma_start(bq[:], b_q).then_inc(bq_in, 16)
            act.wait_ge(bkv_zeroed, 1)
            act.dma_start(bkv[0:1, :], b_kv).then_inc(bkv_in, 16)
            act.dma_start(bkv[32:33, :], b_kv).then_inc(bkv_in, 16)
            act.dma_start(rope_k[:], tab_k).then_inc(tabk_in, 16)
            act.dma_start(mask[:], head_mask).then_inc(mask_in, 16)
            act.dma_start(wo[:], w_o).then_inc(wo_in, 16)
            act.dma_start(bo[:], b_o.to_broadcast([P, D])).then_inc(bo_in, 16)

            def normalise(c):
                act.wait_ge(shift_done, c + 1)
                for t in range(TILES):
                    nc.scalar.activation(xn[:, c, t], xs[:, c, t], ACT.Identity, bias=shift[:, c, t:t + 1],
                                         scale=rstd[:, c, t:t + 1]).then_inc(xn_done, 1)

            def high_xT(c):
                act.wait_ge(xT_made, TILES * (c + 1))
                nc.scalar.activation(xT_hi[:, c % 2], p_x[:], ACT.Copy).then_inc(xT_hi_done, 1)

            def values(c, b):
                act.wait_ge(kv_made, HALVES * (BPC * c + b + 1))
                nc.scalar.activation(v[:, c % 2, HALVES * b:HALVES * (b + 1)],
                                     p_kv[b][:].rearrange("p (t m) -> p t m", t=HALVES)[:, :, D:2 * D],
                                     ACT.Copy).then_inc(v_done, 1)

            def gate(c, j):
                g = HB * c + j
                act.wait_ge(gu_made, g + 1)
                if g >= 2:
                    act.wait_ge(h_done, g - 1)
                nc.scalar.activation(silu[:, g % 2], p_gate[g % 2][:], ACT.Silu, scale=SCALE).then_inc(silu_done, 1)

            def high_h(c, j):
                g = HB * c + j
                act.wait_ge(h_done, g + 1)
                nc.scalar.activation(h_hi[:, c % 2, j], h[:, g % 2], ACT.Copy).then_inc(h_hi_done, 1)

            def products(c):
                act.wait_ge(kvo_made, c + 1)
                pv = p_kv[1][:, 0:BPC * D].rearrange("p (b d) -> p b d", b=BPC)
                nc.scalar.activation(kvo[:], pv, ACT.Copy).then_inc(kvo_done, 1)
                nc.scalar.activation(kvo_swap[0:SWAP], pv[SWAP:D], ACT.Copy).then_inc(kvo_done, 1)
                nc.scalar.activation(kvo_swap[SWAP:D], pv[0:SWAP], ACT.Copy).then_inc(kvo_done, 1)

            act.wait_ge(wqkv_in, 16)
            nc.scalar.activation(wqkv_hi[:], wqkv[:], ACT.Copy).then_inc(wqkv_hi_done, 1)
            normalise(0)
            act.wait_ge(wf_in, 16)
            nc.scalar.activation(wf_hi[:], wf[:], ACT.Copy).then_inc(wf_hi_done, 1)
            high_xT(0)
            values(0, 0)
            values(0, 1)
            normalise(1)
            for c in range(CHUNKS):
                gate(c, 0)
                if c + 1 < CHUNKS:
                    high_xT(c + 1)
                high_h(c, 0)
                gate(c, 1)
                high_h(c, 1)
                gate(c, 2)
                products(c)
                high_h(c, 2)
                if c + 1 < CHUNKS:
                    values(c + 1, 0)
                    values(c + 1, 1)
                if c + 2 < CHUNKS:
                    normalise(c + 2)

        @block.vector
        def _(dve):
            def statistics(c):
                dve.wait_ge(x_in[c], 16)
                for t in range(TILES):
                    nc.vector.bn_stats(bn[:, c, t], xs[:, c, t]).then_inc(bn_done, 1)
                for t in range(TILES):
                    dve.wait_ge(bn_done, TILES * c + t + 1)
                    nc.vector.bn_aggr(mv[:, c, t], bn[:, c, t]).then_inc(mv_done, 1)

            def low_xT(c):
                dve.wait_ge(xT_hi_done, c + 1)
                nc.vector.tensor_tensor(xT_lo[:, c % 2], p_x[:], xT_hi[:, c % 2].bitcast(f32),
                                        ALU.subtract).then_inc(xT_lo_done, 1)

            def rotate_q(c):
                dve.wait_ge(q_made, c + 1)
                for n, dst in enumerate((q_cos, q_sin)):
                    nc.vector.scalar_tensor_tensor(
                        out=dst[:, c % 2].rearrange("p (b l) -> p b l", b=BPC),
                        in0=p_x[:].rearrange("p (b l) -> p b l", b=BPC), scalar=bq[:, 0:1],
                        in1=rope_q[:, n:n + 1, :].to_broadcast([P, BPC, L]),
                        op0=ALU.add, op1=ALU.mult).then_inc(q_rotated, 1)

            def rotate_k(c, b):
                dve.wait_ge(v_done, BPC * c + b + 1)
                t = slice(HALVES * b, HALVES * (b + 1))
                k = p_kv[b][:].rearrange("p (t m) -> p t m", t=HALVES)[:, :, 0:D]
                nc.vector.tensor_tensor(k_cos[:, c % 2, t], k, rope_k[:, 0], ALU.mult).then_inc(k_parts_done, 1)
                for s in range(2):
                    last = nc.vector.tensor_tensor(k_sin[:, c % 2, t, s * SWAP:(s + 1) * SWAP],
                                                   k[:, :, (1 - s) * SWAP:(2 - s) * SWAP],
                                                   rope_k[:, 1, :, s * SWAP:(s + 1) * SWAP], ALU.mult)
                last.then_inc(k_parts_done, 1)

            def hidden(c, j):
                g = HB * c + j
                dve.wait_ge(silu_done, g + 1)
                if g >= 2:
                    dve.wait_ge(h_lo_done, g - 1)
                nc.vector.scalar_tensor_tensor(out=h[:, g % 2], in0=p_up[g % 2][:], scalar=SCALE * SCALE,
                                               in1=silu[:, g % 2], op0=ALU.mult, op1=ALU.mult).then_inc(h_done, 1)

            def keep_heads(c):
                dve.wait_ge(prod_made, c + 1)
                nc.vector.tensor_tensor(kv[:], p_kv[0][:, 0:BPC * D].rearrange("p (b d) -> p b d", b=BPC),
                                        mask[:].rearrange("p (o d) -> p o d", o=1).to_broadcast([P, BPC, D]),
                                        ALU.mult).then_inc(prod_masked, 1)

            def finish(c):
                dve.wait_ge(xres_done, c + 1)
                parts = 2 if c == CHUNKS - 1 else 1
                for s in range(parts):
                    dve.wait_ge(out_made, TILES * c + (s + 1) * TILES // parts)
                    w = slice(s * N // parts, (s + 1) * N // parts)
                    nc.vector.tensor_tensor(outs[:, c, w], out_bank(c, s)[:, w],
                                            xres[:, c].rearrange("p t d -> p (t d)")[:, w],
                                            ALU.add).then_inc(out_added, 1)

            statistics(0)
            dve.wait_ge(wqkv_hi_done, 1)
            nc.vector.tensor_tensor(wqkv_lo[:], wqkv[:], wqkv_hi[:].bitcast(f32),
                                    ALU.subtract).then_inc(wqkv_lo_done, 1)
            dve.wait_ge(bkv_in, 32)
            dve.wait_ge(consts_set, 3)
            nc.vector.tensor_copy(bkv_parts[0:64], bkv[0:64]).then_inc(bkv_hi_done, 1)
            dve.wait_ge(bkv_hi_done, 1)
            nc.vector.tensor_tensor(bkv_parts[32:64], bkv[32:64], bkv_parts[32:64].bitcast(f32),
                                    ALU.subtract).then_inc(bkv_ready, 1)
            statistics(1)
            low_xT(0)
            dve.wait_ge(wf_hi_done, 1)
            nc.vector.tensor_tensor(wf_lo[:], wf[:], wf_hi[:].bitcast(f32), ALU.subtract).then_inc(wf_lo_done, 1)
            dve.wait_ge(bq_in, 16)
            dve.wait_ge(tabq_in, 16)
            rotate_q(0)
            dve.wait_ge(tabk_in, 16)
            rotate_k(0, 0)
            rotate_k(0, 1)
            dve.wait_ge(mask_in, 16)
            for c in range(CHUNKS):
                hidden(c, 0)
                if c + 1 < CHUNKS:
                    low_xT(c + 1)
                hidden(c, 1)
                keep_heads(c)
                if c + 2 < CHUNKS:
                    statistics(c + 2)
                hidden(c, 2)
                if c + 1 < CHUNKS:
                    rotate_q(c + 1)
                    rotate_k(c + 1, 0)
                    rotate_k(c + 1, 1)
                finish(c)

        @block.tensor
        def _(pe):
            def transpose_x(c):
                if c >= 1:
                    pe.wait_ge(q_rotated, 2 * c)
                for t in range(TILES):
                    pe.wait_ge(xn_done, TILES * c + t + 1)
                    nc.tensor.transpose(p_x[:, t * P:(t + 1) * P], xn[:, c, t], ident[:]).then_inc(xT_made, 1)

            def project_q(c):
                pe.wait_ge(xT_lo_done, c + 1)
                xh, xl = xT_hi[:, c % 2], xT_lo[:, c % 2]
                nc.tensor.matmul(p_x[:], wqkv_hi[:, 0:D], xh, start=True, stop=False)
                nc.tensor.matmul(p_x[:], wqkv_hi[:, 0:D], xl, start=False, stop=False)
                nc.tensor.matmul(p_x[:], wqkv_lo[:, 0:D], xh, start=False, stop=True).then_inc(q_made, 1)

            def project_kv(c, b):
                if b == 1 and c >= 1:
                    pe.wait_ge(kvo_done, 3 * c)
                for half in range(HALVES):
                    cols = slice((HALVES * b + half) * P, (HALVES * b + half + 1) * P)
                    dst = p_kv[b][:, half * 2 * D:(half + 1) * 2 * D]
                    xh, xl = xT_hi[:, c % 2, cols], xT_lo[:, c % 2, cols]
                    nc.tensor.matmul(dst, ones[:], bkv_parts[:], start=True, stop=False)
                    nc.tensor.matmul(dst, xh, wqkv_hi[:, D:3 * D], start=False, stop=False)
                    nc.tensor.matmul(dst, xh, wqkv_lo[:, D:3 * D], start=False, stop=False)
                    nc.tensor.matmul(dst, xl, wqkv_hi[:, D:3 * D], start=False, stop=True).then_inc(kv_made, 1)

            def gate_up(c, j):
                g = HB * c + j
                if g >= 2:
                    pe.wait_ge(silu_done, g - 1)
                    pe.wait_ge(h_done, g - 1)
                units = slice(j * P, (j + 1) * P)
                xh, xl = xT_hi[:, c % 2], xT_lo[:, c % 2]
                for m, bank in enumerate((p_gate[g % 2], p_up[g % 2])):
                    nc.tensor.matmul(bank[:], wf_lo[:, m, units], xh, start=True, stop=False)
                    nc.tensor.matmul(bank[:], wf_hi[:, m, units], xh, start=False, stop=False)
                    last = nc.tensor.matmul(bank[:], wf_hi[:, m, units], xl, start=False, stop=True)
                last.then_inc(gu_made, 1)

            def keys_values(c):
                pe.wait_ge(k_rotated, BPC * (c + 1))
                pe.wait_ge(v_done, BPC * (c + 1))
                for b in range(BPC):
                    for half in range(HALVES):
                        t = HALVES * b + half
                        last = nc.tensor.matmul(p_kv[0][:, b * D:(b + 1) * D], v[:, c % 2, t], k_rot[:, c % 2, t],
                                                start=(half == 0), stop=(half == HALVES - 1))
                last.then_inc(prod_made, 1)

            def times_wo(c):
                pe.wait_ge(prod_masked, c + 1)
                for b in range(BPC):
                    last = nc.tensor.matmul(p_kv[1][:, b * D:(b + 1) * D], kv[:, b], wo[:], start=True, stop=True)
                last.then_inc(kvo_made, 1)

            def output(c):
                if c >= 1:
                    pe.wait_ge(out_added, c)
                pe.wait_ge(kvo_done, 3 * (c + 1))
                pe.wait_ge(q_rotated, 2 * (c + 1))
                pe.wait_ge(h_lo_done, HB * (c + 1))
                for t in range(TILES):
                    cols = slice(t * P, (t + 1) * P)
                    b = t // HALVES
                    dst = out_bank(c, b)[:, t * D:(t + 1) * D]
                    nc.tensor.matmul(dst, q_cos[:, c % 2, cols], kvo[:, b], start=True, stop=False)
                    nc.tensor.matmul(dst, q_sin[:, c % 2, cols], kvo_swap[:, b], start=False, stop=False)
                    for j in range(HB):
                        w_hi = wf_hi[:, 2, j * D:(j + 1) * D]
                        w_lo = wf_lo[:, 2, j * D:(j + 1) * D]
                        hh, hl = h_hi[:, c % 2, j, cols], h_lo[:, c % 2, j, cols]
                        nc.tensor.matmul(dst, hh, w_hi, start=False, stop=False)
                        nc.tensor.matmul(dst, hh, w_lo, start=False, stop=False)
                        last = nc.tensor.matmul(dst, hl, w_hi, start=False, stop=(j == HB - 1))
                    last.then_inc(out_made, 1)

            pe.wait_ge(ident_in, 16)
            transpose_x(0)
            pe.wait_ge(wqkv_lo_done, 1)
            project_q(0)
            pe.wait_ge(bkv_ready, 1)
            project_kv(0, 0)
            project_kv(0, 1)
            pe.wait_ge(wf_lo_done, 1)
            pe.wait_ge(wo_in, 16)
            for c in range(CHUNKS):
                gate_up(c, 0)
                if c + 1 < CHUNKS:
                    transpose_x(c + 1)
                gate_up(c, 1)
                keys_values(c)
                gate_up(c, 2)
                times_wo(c)
                if c + 1 < CHUNKS:
                    project_q(c + 1)
                    project_kv(c + 1, 0)
                    project_kv(c + 1, 1)
                output(c)


def kernel(L0_attn_x, L0_attn_Wq, L0_attn_bq, L0_attn_Wk, L0_attn_bk, L0_attn_Wv, L0_attn_bv, L0_attn_Wo,
           L0_attn_bo, L0_ffn_w_gate, L0_ffn_w_up, L0_ffn_w_down):
    import numpy as np
    import concourse.bacc as bacc
    from concourse.bass_utils import run_bass_kernel_spmd

    f = np.float32
    part, pair, head = np.meshgrid(np.arange(2), np.arange(PAIRS), np.arange(HEADS), indexing="ij")
    order = (head * HD + 2 * pair + part).ravel()
    part, pair, head = part.ravel(), pair.ravel(), head.ravel()
    freqs = (f(1.0) / np.power(f(10000.0), np.arange(0, HD, 2, dtype=f))).astype(f)
    angles = (np.arange(L, dtype=f)[:, None] * freqs[None, :]).astype(f)
    cos, sin = np.cos(angles)[:, pair].astype(f), np.sin(angles)[:, pair].astype(f)
    sign = np.where(part == 0, f(1), f(-1))
    tab_k = np.stack([cos.reshape(P, HALVES, D), (-sign * sin).reshape(P, HALVES, D)], 1)
    tile_order = np.arange(L).reshape(P, HALVES).T.ravel()
    tab_q = np.stack([cos[tile_order].T, (sign * sin)[tile_order].T], 1)
    head_mask = np.where(np.arange(D)[:, None] // HD == head[None, :], f(1.0 / np.sqrt(HD)), f(0)).astype(f)

    a = {k: np.asarray(t) for k, t in dict(
        x=L0_attn_x, wq=L0_attn_Wq, wk=L0_attn_Wk, wv=L0_attn_Wv, wo=L0_attn_Wo, bq=L0_attn_bq, bk=L0_attn_bk,
        bv=L0_attn_bv, bo=L0_attn_bo, wg=L0_ffn_w_gate, wu=L0_ffn_w_up, wd=L0_ffn_w_down).items()}
    arrays = {
        "x": a["x"],
        "w_qkv": np.concatenate([a["wq"][:, order], a["wk"][:, order], a["wv"]], 1),
        "w_o": a["wo"],
        "b_q": a["bq"][order][:, None],
        "b_kv": np.concatenate([a["bk"][order], a["bv"]])[None, :],
        "b_o": a["bo"][None, :],
        "w_ffn": np.stack([a["wg"].T, a["wu"].T,
                           a["wd"].T.reshape(HB, P, D).transpose(1, 0, 2).reshape(P, HIDDEN)], 1),
        "tab_k": tab_k, "tab_q": tab_q, "head_mask": head_mask, "identity": np.eye(P, dtype=f),
    }
    arrays = {k: np.ascontiguousarray(t) for k, t in arrays.items()}
    nc = bacc.Bacc("TRN2", target_bir_lowering=False, num_devices=1)
    args = [nc.dram_tensor(k, t.shape, mybir.dt.from_np(t.dtype), kind="ExternalInput").ap() for k, t in arrays.items()]
    args.append(nc.dram_tensor("out", (B, L, D), mybir.dt.float32, kind="ExternalOutput").ap())
    build(nc, *args)
    r = run_bass_kernel_spmd(nc, [arrays], core_ids=[0])
    return r.results[0]["out"]
```

```python
import concourse.bass as bass
from concourse import mybir
from contextlib import ExitStack

P = 128
B, L, D = 8, 256, 128
HEADS, HD = 16, 8
PAIRS = HD // 2
HIDDEN = 384
HB = HIDDEN // P
BPC = 2
CHUNKS = B // BPC
HALVES = L // P
TILES = BPC * HALVES
N = TILES * P
SWAP = D // 2
SCALE = 1.0 / 127.0
EPS = 1e-5
EXACT = 1 << 12
WARM_UP, WARM_BETWEEN = 16, 7


def build(nc, x, early, w_ffn, rope, late, out):
    f32, f32r, i32 = mybir.dt.float32, mybir.dt.float32r, mybir.dt.int32
    ALU = mybir.AluOpType
    ACT = mybir.ActivationFunctionType

    ctx = ExitStack()
    with ctx:
        def sb(name, shape, dt=f32):
            return ctx.enter_context(nc.sbuf_tensor(name, shape, dt))

        def pb(name):
            return ctx.enter_context(nc.psum_tensor(name, [P, N], f32))

        def sem(name):
            return ctx.enter_context(nc.semaphore(name))

        first = sb("first", [P, P + 3 * D + 2 * D + 2])
        ident = first[:, 0:P]
        wqkv = first[:, P:P + 3 * D]
        bkv = first[:, P + 3 * D:P + 5 * D]
        bq = first[:, P + 5 * D:P + 5 * D + 1]
        bo = first[:, P + 5 * D + 1:P + 5 * D + 2]
        tables = sb("tables", [P, 4 * L])
        rope_k = tables[:, 0:2 * L].rearrange("p (n h d) -> p n h d", n=2, h=HALVES)
        rope_q = tables[:, 2 * L:4 * L].rearrange("p (n l) -> p n l", n=2)
        last = sb("last", [P, 2 * D])
        mask = last[:, 0:D]
        wo = last[:, D:2 * D]
        wqkv_hi = sb("wqkv_hi", [P, 3 * D], f32r)
        wqkv_lo = sb("wqkv_lo", [P, 3 * D], f32r)
        bkv_parts = sb("bkv_parts", [P, 2 * D], f32r)
        ones = sb("ones", [P, P], f32r)
        wf = sb("wf", [P, 3, HIDDEN], i32)
        wf_hi = sb("wf_hi", [P, 3, HIDDEN], f32r)
        wf_lo = sb("wf_lo", [P, 3, HIDDEN], f32r)
        largest = sb("largest", [P, 1])
        largest_all = sb("largest_all", [1, 1], i32)
        warm = sb("warm", [P, N], mybir.dt.bfloat16)
        xs = sb("xs", [P, CHUNKS, TILES, D])
        oT = sb("oT", [P, 2, N])
        xn = sb("xn", [P, CHUNKS, TILES, D])
        outs = sb("outs", [P, CHUNKS, TILES * D])
        bn = sb("bn", [P, CHUNKS, TILES, 6])
        mv = sb("mv", [P, CHUNKS, TILES, 2])
        minus_half = sb("minus_half", [P, TILES])
        veps = sb("veps", [P, CHUNKS, TILES])
        rstd = sb("rstd", [P, CHUNKS, TILES])
        shift = sb("shift", [P, CHUNKS, TILES])
        xT_hi = sb("xT_hi", [P, 2, N], f32r)
        xT_lo = sb("xT_lo", [P, 2, N], f32r)
        q_cos = sb("q_cos", [P, 2, N])
        q_sin = sb("q_sin", [P, 2, N])
        k_cos = sb("k_cos", [P, 2, TILES, D])
        k_sin = sb("k_sin", [P, 2, TILES, D])
        k_rot = sb("k_rot", [P, 2, TILES, D])
        v = sb("v", [P, 2, TILES, D])
        kv = sb("kv", [P, BPC, D])
        kvo = sb("kvo", [P, BPC, D])
        kvo_swap = sb("kvo_swap", [P, BPC, D])
        silu = sb("silu", [P, 2, N])
        h = sb("h", [P, 2, N])
        h_hi = sb("h_hi", [P, 2, HB, N], f32r)
        h_lo = sb("h_lo", [P, 2, HB, N], f32r)

        p_gate = [pb("p_gate0"), pb("p_gate1")]
        p_up = [pb("p_up0"), pb("p_up1")]
        p_x = pb("p_x")
        p_kv = [pb("p_kv0"), pb("p_kv1")]
        p_out = pb("p_out")

        def sum_bank(c, b):
            return p_x if c == CHUNKS - 1 and b == 1 else p_out

        def back_bank(c, b):
            return p_kv[b] if c == CHUNKS - 1 else p_out

        x_in = [sem(f"x_in{c}") for c in range(CHUNKS)]
        first_in, wf_in, tables_in, last_in = (sem(n) for n in ("first_in", "wf_in", "tables_in", "last_in"))
        out_done = sem("out_done")
        consts_set = sem("consts_set")
        warm_set = sem("warm_set")
        table_loaded = sem("table_loaded")
        bkv_hi_done = sem("bkv_hi_done")
        bkv_ready = sem("bkv_ready")
        wqkv_hi_done = sem("wqkv_hi_done")
        wqkv_lo_done = sem("wqkv_lo_done")
        wf_hi_done = sem("wf_hi_done")
        wf_lo_done = sem("wf_lo_done")
        bn_done = sem("bn_done")
        mv_done = sem("mv_done")
        veps_done = sem("veps_done")
        rstd_done = sem("rstd_done")
        shift_done = sem("shift_done")
        xn_done = sem("xn_done")
        xn_first = sem("xn_first")
        largest_done = sem("largest_done")
        largest_turned = sem("largest_turned")
        largest_all_done = sem("largest_all_done")
        xT_made = sem("xT_made")
        xT_hi_done = sem("xT_hi_done")
        xT_lo_done = sem("xT_lo_done")
        q_made = sem("q_made")
        q_rotated = sem("q_rotated")
        kv_made = sem("kv_made")
        v_done = sem("v_done")
        k_parts_done = sem("k_parts_done")
        k_rotated = sem("k_rotated")
        prod_made = sem("prod_made")
        prod_masked = sem("prod_masked")
        kvo_made = sem("kvo_made")
        kvo_done = sem("kvo_done")
        gu_made = sem("gu_made")
        silu_done = sem("silu_done")
        h_done = sem("h_done")
        h_hi_done = sem("h_hi_done")
        h_lo_done = sem("h_lo_done")
        sum_made = sem("sum_made")
        sum_done = sem("sum_done")
        out_turned = sem("out_turned")
        out_added = sem("out_added")

        block = ctx.enter_context(nc.Block())

        x_view = x.rearrange("(c b) (p h) d -> c p b (h d)", b=BPC, h=HALVES)
        out_view = out.rearrange("(c b) (p h) d -> c p b (h d)", b=BPC, h=HALVES)

        @block.sync
        def _(sp):
            def load_x(c):
                sp.dma_start(xs[:, c].rearrange("p (b h) d -> p b (h d)", b=BPC), x_view[c]).then_inc(x_in[c], 16)

            load_x(0)
            sp.dma_start(first[:], early).then_inc(first_in, 16)
            sp.dma_start(wf[:], w_ffn).then_inc(wf_in, 16)
            sp.dma_start(tables[:], rope).then_inc(tables_in, 16)
            load_x(1)
            sp.dma_start(last[:], late).then_inc(last_in, 16)
            load_x(2)
            load_x(3)
            for c in range(CHUNKS):
                parts = BPC if c == CHUNKS - 1 else 1
                for s in range(parts):
                    sp.wait_ge(out_added, c + s + 1)
                    b = slice(s * BPC // parts, (s + 1) * BPC // parts)
                    sp.dma_start(out_view[c][:, b], outs[:, c].rearrange("p (b m) -> p b m", b=BPC)[:, b]
                                 ).then_inc(out_done, 16)
            sp.wait_ge(out_done, 16 * (CHUNKS - 1 + BPC))

        @block.gpsimd
        def _(pool):
            nc.gpsimd.memset(warm[:], 0.0).then_inc(warm_set, 1)
            nc.gpsimd.memset(minus_half[:], -0.5).then_inc(consts_set, 1)
            nc.gpsimd.memset(ones[:].bitcast(f32), 1.0).then_inc(consts_set, 1)
            nc.gpsimd.memset(bkv_parts[:].bitcast(f32), 0.0).then_inc(consts_set, 1)

            def spread(c):
                pool.wait_ge(veps_done, c + 1)
                if c == 0:
                    pool.wait_ge(consts_set, 1)
                nc.gpsimd.tensor_tensor(rstd[:, c], veps[:, c], minus_half[:], ALU.pow).then_inc(rstd_done, 1)

            def rotate_k(c, b):
                pool.wait_ge(k_parts_done, 2 * (BPC * c + b + 1))
                t = slice(HALVES * b, HALVES * (b + 1))
                nc.gpsimd.tensor_tensor(k_rot[:, c % 2, t], k_cos[:, c % 2, t], k_sin[:, c % 2, t],
                                        ALU.add).then_inc(k_rotated, 1)

            def low_h(c, j):
                g = HB * c + j
                pool.wait_ge(h_hi_done, g + 1)
                nc.gpsimd.tensor_tensor(h_lo[:, c % 2, j], h[:, g % 2], h_hi[:, c % 2, j].bitcast(f32),
                                        ALU.subtract).then_inc(h_lo_done, 1)

            spread(0)
            spread(1)
            rotate_k(0, 0)
            rotate_k(0, 1)
            for c in range(CHUNKS):
                low_h(c, 0)
                if c + 2 < CHUNKS:
                    spread(c + 2)
                low_h(c, 1)
                low_h(c, 2)
                if c + 1 < CHUNKS:
                    rotate_k(c + 1, 0)
                    rotate_k(c + 1, 1)

        @block.scalar
        def _(act):
            act.wait_ge(warm_set, 1)
            nc.scalar.activation(silu[:, 0, 0:1], warm[:, 0:1], ACT.Silu).then_inc(table_loaded, 1)

            def normalise(c, tiles):
                act.wait_ge(shift_done, c + 1)
                for t in tiles:
                    nc.scalar.activation(xn[:, c, t], xs[:, c, t], ACT.Identity, bias=shift[:, c, t:t + 1],
                                         scale=rstd[:, c, t:t + 1]).then_inc(xn_done, 1)

            def high_xT(c):
                act.wait_ge(xT_made, TILES * (c + 1))
                nc.scalar.activation(xT_hi[:, c % 2], p_x[:], ACT.Copy).then_inc(xT_hi_done, 1)

            def values(c, b):
                act.wait_ge(kv_made, HALVES * (BPC * c + b + 1))
                nc.scalar.activation(v[:, c % 2, HALVES * b:HALVES * (b + 1)],
                                     p_kv[b][:].rearrange("p (t m) -> p t m", t=HALVES)[:, :, D:2 * D],
                                     ACT.Copy).then_inc(v_done, 1)

            def gate(c, j):
                g = HB * c + j
                act.wait_ge(gu_made, g + 1)
                if g >= 2:
                    act.wait_ge(h_done, g - 1)
                nc.scalar.activation(silu[:, g % 2], p_gate[g % 2][:], ACT.Silu, scale=SCALE).then_inc(silu_done, 1)

            def high_h(c, j):
                g = HB * c + j
                act.wait_ge(h_done, g + 1)
                nc.scalar.activation(h_hi[:, c % 2, j], h[:, g % 2], ACT.Copy).then_inc(h_hi_done, 1)

            def products(c):
                act.wait_ge(kvo_made, c + 1)
                pv = p_kv[1][:, 0:BPC * D].rearrange("p (b d) -> p b d", b=BPC)
                nc.scalar.activation(kvo[:], pv, ACT.Copy).then_inc(kvo_done, 1)
                nc.scalar.activation(kvo_swap[0:SWAP], pv[SWAP:D], ACT.Copy).then_inc(kvo_done, 1)
                nc.scalar.activation(kvo_swap[SWAP:D], pv[0:SWAP], ACT.Copy).then_inc(kvo_done, 1)

            def summed(c, b, n):
                act.wait_ge(sum_made, (BPC * c + b + n))
                w = slice(b * L, (b + n) * L)
                nc.scalar.activation(oT[:, c % 2, w], sum_bank(c, b)[:, w], ACT.Identity,
                                     bias=bo).then_inc(sum_done, n)

            act.wait_ge(first_in, 16)
            nc.scalar.activation(wqkv_hi[:], wqkv, ACT.Copy).then_inc(wqkv_hi_done, 1)
            normalise(0, (2, 3))
            high_xT(0)
            act.wait_ge(wf_in, 16)
            nc.scalar.activation(wf_hi[:], wf[:], ACT.Copy).then_inc(wf_hi_done, 1)
            values(0, 0)
            values(0, 1)
            normalise(1, range(TILES))
            for c in range(CHUNKS):
                gate(c, 0)
                high_h(c, 0)
                if c + 1 < CHUNKS:
                    high_xT(c + 1)
                gate(c, 1)
                high_h(c, 1)
                if c >= 1:
                    summed(c - 1, 0, BPC)
                gate(c, 2)
                high_h(c, 2)
                products(c)
                if c + 1 < CHUNKS:
                    values(c + 1, 0)
                    values(c + 1, 1)
                if c + 2 < CHUNKS:
                    normalise(c + 2, range(TILES))
            for b in range(BPC):
                summed(CHUNKS - 1, b, 1)

        @block.vector
        def _(dve):
            def statistics(c):
                dve.wait_ge(x_in[c], 16)
                for t in range(TILES):
                    nc.vector.bn_stats(bn[:, c, t], xs[:, c, t]).then_inc(bn_done, 1)
                for t in range(TILES):
                    dve.wait_ge(bn_done, TILES * c + t + 1)
                    nc.vector.bn_aggr(mv[:, c, t], bn[:, c, t]).then_inc(mv_done, 1)

            def spread(c):
                dve.wait_ge(mv_done, TILES * (c + 1))
                nc.vector.tensor_scalar(veps[:, c], mv[:, c, :, 1], EPS, None, ALU.add).then_inc(veps_done, 1)

            def shifts(c):
                dve.wait_ge(rstd_done, c + 1)
                nc.vector.scalar_tensor_tensor(out=shift[:, c], in0=mv[:, c, :, 0], scalar=-1.0, in1=rstd[:, c],
                                               op0=ALU.mult, op1=ALU.mult).then_inc(shift_done, 1)

            def low_xT(c):
                dve.wait_ge(xT_hi_done, c + 1)
                nc.vector.tensor_tensor(xT_lo[:, c % 2], p_x[:], xT_hi[:, c % 2].bitcast(f32),
                                        ALU.subtract).then_inc(xT_lo_done, 1)

            def rotate_q(c):
                dve.wait_ge(q_made, c + 1)
                for n, dst in enumerate((q_cos, q_sin)):
                    nc.vector.scalar_tensor_tensor(
                        out=dst[:, c % 2].rearrange("p (b l) -> p b l", b=BPC),
                        in0=p_x[:].rearrange("p (b l) -> p b l", b=BPC), scalar=bq,
                        in1=rope_q[:, n:n + 1, :].to_broadcast([P, BPC, L]),
                        op0=ALU.add, op1=ALU.mult).then_inc(q_rotated, 1)

            def rotate_k(c, b):
                dve.wait_ge(v_done, BPC * c + b + 1)
                t = slice(HALVES * b, HALVES * (b + 1))
                k = p_kv[b][:].rearrange("p (t m) -> p t m", t=HALVES)[:, :, 0:D]
                nc.vector.tensor_tensor(k_cos[:, c % 2, t], k, rope_k[:, 0], ALU.mult).then_inc(k_parts_done, 1)
                for s in range(2):
                    final = nc.vector.tensor_tensor(k_sin[:, c % 2, t, s * SWAP:(s + 1) * SWAP],
                                                   k[:, :, (1 - s) * SWAP:(2 - s) * SWAP],
                                                   rope_k[:, 1, :, s * SWAP:(s + 1) * SWAP], ALU.mult)
                final.then_inc(k_parts_done, 1)

            def hidden(c, j):
                g = HB * c + j
                dve.wait_ge(silu_done, g + 1)
                if g >= 2:
                    dve.wait_ge(h_lo_done, g - 1)
                nc.vector.scalar_tensor_tensor(out=h[:, g % 2], in0=p_up[g % 2][:], scalar=SCALE * SCALE,
                                               in1=silu[:, g % 2], op0=ALU.mult, op1=ALU.mult).then_inc(h_done, 1)

            def keep_heads(c):
                dve.wait_ge(prod_made, c + 1)
                nc.vector.tensor_tensor(kv[:], p_kv[0][:, 0:BPC * D].rearrange("p (b d) -> p b d", b=BPC),
                                        mask.rearrange("p (o d) -> p o d", o=1).to_broadcast([P, BPC, D]),
                                        ALU.mult).then_inc(prod_masked, 1)

            def finish(c, b, n):
                dve.wait_ge(out_turned, BPC * c + b + n)
                w = slice(b * L, (b + n) * L)
                nc.vector.tensor_tensor(outs[:, c, w], back_bank(c, b)[:, w],
                                        xs[:, c].rearrange("p t d -> p (t d)")[:, w], ALU.add).then_inc(out_added, 1)

            statistics(0)
            spread(0)
            dve.wait_ge(wqkv_hi_done, 1)
            nc.vector.tensor_tensor(wqkv_lo[:], wqkv, wqkv_hi[:].bitcast(f32),
                                    ALU.subtract).then_inc(wqkv_lo_done, 1)
            shifts(0)
            for t in (0, 1):
                nc.vector.tensor_scalar(xn[:, 0, t], xs[:, 0, t], mv[:, 0, t, 0:1], rstd[:, 0, t:t + 1],
                                        ALU.subtract, ALU.mult).then_inc(xn_first, 1)
            dve.wait_ge(consts_set, 3)
            nc.vector.tensor_copy(bkv_parts[0:64], bkv[0:64]).then_inc(bkv_hi_done, 1)
            dve.wait_ge(bkv_hi_done, 1)
            nc.vector.tensor_tensor(bkv_parts[32:64], bkv[32:64], bkv_parts[32:64].bitcast(f32),
                                    ALU.subtract).then_inc(bkv_ready, 1)
            dve.wait_ge(wf_in, 16)
            nc.vector.tensor_reduce(largest[:], wf[:], mybir.AxisListType.XY, ALU.max,
                                    apply_absolute_value=True).then_inc(largest_done, 1)
            low_xT(0)
            dve.wait_ge(largest_turned, 1)
            nc.vector.tensor_reduce(largest_all[:], p_out[0:1, 0:P], mybir.AxisListType.X,
                                    ALU.max).then_inc(largest_all_done, 1)
            dve.wait_ge(tables_in, 16)
            rotate_q(0)
            statistics(1)
            spread(1)
            rotate_k(0, 0)
            rotate_k(0, 1)
            shifts(1)
            dve.wait_ge(wf_hi_done, 1)
            nc.vector.tensor_tensor(wf_lo[:], wf[:], wf_hi[:].bitcast(f32), ALU.subtract).then_inc(wf_lo_done, 1)
            dve.wait_ge(last_in, 16)
            for c in range(CHUNKS):
                hidden(c, 0)
                if c + 1 < CHUNKS:
                    low_xT(c + 1)
                hidden(c, 1)
                if c + 2 < CHUNKS:
                    statistics(c + 2)
                    spread(c + 2)
                keep_heads(c)
                hidden(c, 2)
                if c >= 1:
                    finish(c - 1, 0, BPC)
                if c + 1 < CHUNKS:
                    rotate_q(c + 1)
                    if c + 2 < CHUNKS:
                        shifts(c + 2)
                    rotate_k(c + 1, 0)
                    rotate_k(c + 1, 1)
            for b in range(BPC):
                finish(CHUNKS - 1, b, 1)

        @block.tensor
        def _(pe):
            def transpose_x(c):
                if c >= 1:
                    pe.wait_ge(q_rotated, 2 * c)
                for t in range(TILES):
                    if c == 0 and t < 2:
                        pe.wait_ge(xn_first, t + 1)
                    else:
                        pe.wait_ge(xn_done, TILES * c + t - 1)
                    nc.tensor.transpose(p_x[:, t * P:(t + 1) * P], xn[:, c, t], ident).then_inc(xT_made, 1)

            def project_q(c):
                pe.wait_ge(xT_lo_done, c + 1)
                xh, xl = xT_hi[:, c % 2], xT_lo[:, c % 2]
                nc.tensor.matmul(p_x[:], wqkv_hi[:, 0:D], xh, start=True, stop=False)
                nc.tensor.matmul(p_x[:], wqkv_hi[:, 0:D], xl, start=False, stop=False)
                nc.tensor.matmul(p_x[:], wqkv_lo[:, 0:D], xh, start=False, stop=True).then_inc(q_made, 1)

            def project_kv(c, b):
                if b == 1 and c >= 1:
                    pe.wait_ge(kvo_done, 3 * c)
                for half in range(HALVES):
                    cols = slice((HALVES * b + half) * P, (HALVES * b + half + 1) * P)
                    dst = p_kv[b][:, half * 2 * D:(half + 1) * 2 * D]
                    xh, xl = xT_hi[:, c % 2, cols], xT_lo[:, c % 2, cols]
                    nc.tensor.matmul(dst, ones[:], bkv_parts[:], start=True, stop=False)
                    nc.tensor.matmul(dst, xh, wqkv_hi[:, D:3 * D], start=False, stop=False)
                    nc.tensor.matmul(dst, xh, wqkv_lo[:, D:3 * D], start=False, stop=False)
                    nc.tensor.matmul(dst, xl, wqkv_hi[:, D:3 * D], start=False, stop=True).then_inc(kv_made, 1)

            def gate_up(c, j, low):
                g = HB * c + j
                if g >= 2:
                    pe.wait_ge(silu_done, g - 1)
                    pe.wait_ge(h_done, g - 1)
                units = slice(j * P, (j + 1) * P)
                xh, xl = xT_hi[:, c % 2], xT_lo[:, c % 2]
                for m, bank in enumerate((p_gate[g % 2], p_up[g % 2])):
                    nc.tensor.matmul(bank[:], wf_hi[:, m, units], xh, start=True, stop=False)
                    if low:
                        nc.tensor.matmul(bank[:], wf_lo[:, m, units], xh, start=False, stop=False)
                    final = nc.tensor.matmul(bank[:], wf_hi[:, m, units], xl, start=False, stop=True)
                final.then_inc(gu_made, 1)

            def keys_values(c):
                pe.wait_ge(k_rotated, BPC * (c + 1))
                pe.wait_ge(v_done, BPC * (c + 1))
                for b in range(BPC):
                    for half in range(HALVES):
                        t = HALVES * b + half
                        final = nc.tensor.matmul(p_kv[0][:, b * D:(b + 1) * D], v[:, c % 2, t], k_rot[:, c % 2, t],
                                                start=(half == 0), stop=(half == HALVES - 1))
                final.then_inc(prod_made, 1)

            def times_wo(c):
                pe.wait_ge(prod_masked, c + 1)
                for b in range(BPC):
                    final = nc.tensor.matmul(p_kv[1][:, b * D:(b + 1) * D], kv[:, b], wo, start=True, stop=True)
                final.then_inc(kvo_made, 1)

            def attended(c, b):
                cols = slice(b * L, (b + 1) * L)
                dst = sum_bank(c, b)[:, cols]
                nc.tensor.matmul(dst, kvo[:, b], q_cos[:, c % 2, cols], start=True, stop=False)
                nc.tensor.matmul(dst, kvo_swap[:, b], q_sin[:, c % 2, cols], start=False, stop=False)

            def down(c, b, j, low):
                cols = slice(b * L, (b + 1) * L)
                dst = sum_bank(c, b)[:, cols]
                w_hi, w_lo = wf_hi[:, 2, j * D:(j + 1) * D], wf_lo[:, 2, j * D:(j + 1) * D]
                hh, hl = h_hi[:, c % 2, j, cols], h_lo[:, c % 2, j, cols]
                nc.tensor.matmul(dst, w_hi, hh, start=False, stop=False)
                if low:
                    nc.tensor.matmul(dst, w_lo, hh, start=False, stop=False)
                final = nc.tensor.matmul(dst, w_hi, hl, start=False, stop=(j == HB - 1))
                if j == HB - 1:
                    final.then_inc(sum_made, 1)

            def sums(c, low):
                if c >= 1:
                    pe.wait_ge(out_added, c)
                pe.wait_ge(kvo_done, 3 * (c + 1))
                pe.wait_ge(q_rotated, 2 * (c + 1))
                if c < CHUNKS - 1:
                    pe.wait_ge(h_lo_done, HB * (c + 1))
                    for b in range(BPC):
                        attended(c, b)
                        for j in range(HB):
                            down(c, b, j, low)
                else:
                    for b in range(BPC):
                        attended(c, b)
                    for j in range(HB):
                        pe.wait_ge(h_lo_done, HB * c + j + 1)
                        for b in range(BPC):
                            down(c, b, j, low)

            def turn_back(c):
                for b in range(BPC):
                    pe.wait_ge(sum_done, BPC * c + (b + 1 if c == CHUNKS - 1 else BPC))
                    for t in range(HALVES * b, HALVES * (b + 1)):
                        cols = slice(t * P, (t + 1) * P)
                        final = nc.tensor.transpose(back_bank(c, b)[:, cols], oT[:, c % 2, cols], ident)
                    final.then_inc(out_turned, 1)

            def warm_up(n):
                for _ in range(n):
                    nc.tensor.matmul(p_out[:], warm[:, 0:P], warm[:], start=True, stop=True)

            def chunks(low):
                for c in range(CHUNKS):
                    if c == 0:
                        gate_up_rest(low)
                    else:
                        gate_up(c, 0, low)
                    if c + 1 < CHUNKS:
                        transpose_x(c + 1)
                    gate_up(c, 1, low)
                    if c > 0:
                        sums(c - 1, low)
                    keys_values(c)
                    gate_up(c, 2, low)
                    times_wo(c)
                    if c > 0:
                        turn_back(c - 1)
                    if c + 1 < CHUNKS:
                        project_q(c + 1)
                        project_kv(c + 1, 0)
                        project_kv(c + 1, 1)
                sums(CHUNKS - 1, low)
                turn_back(CHUNKS - 1)

            def gate_up_begun():
                nc.tensor.matmul(p_gate[0][:], wf_hi[:, 0, 0:P], xT_hi[:, 0], start=True, stop=False)
                nc.tensor.matmul(p_up[0][:], wf_hi[:, 1, 0:P], xT_hi[:, 0], start=True, stop=False)

            def gate_up_rest(low):
                if low:
                    pe.wait_ge(wf_lo_done, 1)
                    nc.tensor.matmul(p_gate[0][:], wf_lo[:, 0, 0:P], xT_hi[:, 0], start=False, stop=False)
                    nc.tensor.matmul(p_up[0][:], wf_lo[:, 1, 0:P], xT_hi[:, 0], start=False, stop=False)
                nc.tensor.matmul(p_gate[0][:], wf_hi[:, 0, 0:P], xT_lo[:, 0], start=False, stop=True)
                nc.tensor.matmul(p_up[0][:], wf_hi[:, 1, 0:P], xT_lo[:, 0], start=False, stop=True).then_inc(gu_made, 1)

            pe.wait_ge(warm_set, 1)
            warm_up(WARM_UP)
            pe.wait_ge(first_in, 16)
            transpose_x(0)
            warm_up(WARM_BETWEEN)
            pe.wait_ge(wqkv_lo_done, 1)
            project_q(0)
            pe.wait_ge(largest_done, 1)
            nc.tensor.transpose(p_out[0:1, 0:P], largest[:], ident).then_inc(largest_turned, 1)
            pe.wait_ge(bkv_ready, 1)
            project_kv(0, 0)
            project_kv(0, 1)
            pe.wait_ge(wf_hi_done, 1)
            gate_up_begun()
            pe.wait_ge(last_in, 16)
            pe.wait_ge(largest_all_done, 1)
            weight = pe.value_load(largest_all[0:1, 0:1])
            with pe.If(weight > EXACT):
                chunks(True)
            with pe.Else():
                chunks(False)


def kernel(L0_attn_x, L0_attn_Wq, L0_attn_bq, L0_attn_Wk, L0_attn_bk, L0_attn_Wv, L0_attn_bv, L0_attn_Wo,
           L0_attn_bo, L0_ffn_w_gate, L0_ffn_w_up, L0_ffn_w_down):
    import numpy as np
    import concourse.bacc as bacc
    from concourse.bass_utils import run_bass_kernel_spmd

    f = np.float32
    part, pair, head = np.meshgrid(np.arange(2), np.arange(PAIRS), np.arange(HEADS), indexing="ij")
    order = (head * HD + 2 * pair + part).ravel()
    part, pair, head = part.ravel(), pair.ravel(), head.ravel()
    freqs = (f(1.0) / np.power(f(10000.0), np.arange(0, HD, 2, dtype=f))).astype(f)
    angles = (np.arange(L, dtype=f)[:, None] * freqs[None, :]).astype(f)
    cos, sin = np.cos(angles)[:, pair].astype(f), np.sin(angles)[:, pair].astype(f)
    sign = np.where(part == 0, f(1), f(-1))
    tab_k = np.stack([cos.reshape(P, HALVES, D), (-sign * sin).reshape(P, HALVES, D)], 1)
    tile_order = np.arange(L).reshape(P, HALVES).T.ravel()
    tab_q = np.stack([cos[tile_order].T, (sign * sin)[tile_order].T], 1)
    head_mask = np.where(np.arange(D)[:, None] // HD == head[None, :], f(1.0 / np.sqrt(HD)), f(0)).astype(f)

    a = {k: np.asarray(t) for k, t in dict(
        x=L0_attn_x, wq=L0_attn_Wq, wk=L0_attn_Wk, wv=L0_attn_Wv, wo=L0_attn_Wo, bq=L0_attn_bq, bk=L0_attn_bk,
        bv=L0_attn_bv, bo=L0_attn_bo, wg=L0_ffn_w_gate, wu=L0_ffn_w_up, wd=L0_ffn_w_down).items()}
    bias_rows = np.zeros((P, 2 * D), f)
    bias_rows[[0, 32]] = np.concatenate([a["bk"][order], a["bv"]])
    arrays = {
        "x": a["x"],
        "early": np.concatenate([np.eye(P, dtype=f), a["wq"][:, order], a["wk"][:, order], a["wv"], bias_rows,
                                 a["bq"][order][:, None], a["bo"][:, None]], 1),
        "w_ffn": np.stack([a["wg"].T, a["wu"].T,
                           a["wd"].T.reshape(HB, P, D).transpose(1, 0, 2).reshape(P, HIDDEN)], 1),
        "rope": np.concatenate([tab_k.reshape(P, -1), tab_q.reshape(P, -1)], 1),
        "late": np.concatenate([head_mask, a["wo"]], 1),
    }
    arrays = {k: np.ascontiguousarray(t) for k, t in arrays.items()}
    nc = bacc.Bacc("TRN2", target_bir_lowering=False, num_devices=1)
    args = [nc.dram_tensor(k, t.shape, mybir.dt.from_np(t.dtype), kind="ExternalInput").ap() for k, t in arrays.items()]
    args.append(nc.dram_tensor("out", (B, L, D), mybir.dt.float32, kind="ExternalOutput").ap())
    build(nc, *args)
    r = run_bass_kernel_spmd(nc, [arrays], core_ids=[0])
    return r.results[0]["out"]
```

```python
import numpy as np
import concourse.bass as bass
from concourse import mybir
from contextlib import ExitStack

P = 128
B, L, D = 8, 256, 128
HEADS, HD = 16, 8
PAIRS = HD // 2
HIDDEN = 384
HB = HIDDEN // P
BPC = 2
CHUNKS = B // BPC
HALVES = L // P
TILES = BPC * HALVES
N = TILES * P
SWAP = D // 2
SCALE = 1.0 / 127.0
EPS = 1e-5
EXACT = 1 << 12
EXACT_BITS = int(np.float32(EXACT).view(np.int32))
WARM_UP, WARM_BETWEEN = 13, 4


def build(nc, x, early, w_ffn, rope, late, out):
    f32, f32r, i32 = mybir.dt.float32, mybir.dt.float32r, mybir.dt.int32
    ALU = mybir.AluOpType
    ACT = mybir.ActivationFunctionType

    ctx = ExitStack()
    with ctx:
        def sb(name, shape, dt=f32):
            return ctx.enter_context(nc.sbuf_tensor(name, shape, dt))

        def pb(name):
            return ctx.enter_context(nc.psum_tensor(name, [P, N], f32))

        def sem(name):
            return ctx.enter_context(nc.semaphore(name))

        first = sb("first", [P, P + 3 * D + 2 * D + 2])
        ident = first[:, 0:P]
        wqkv = first[:, P:P + 3 * D]
        bkv = first[:, P + 3 * D:P + 5 * D]
        bq = first[:, P + 5 * D:P + 5 * D + 1]
        bo = first[:, P + 5 * D + 1:P + 5 * D + 2]
        tables = sb("tables", [P, 4 * L])
        rope_k = tables[:, 0:2 * L].rearrange("p (n h d) -> p n h d", n=2, h=HALVES)
        rope_q = tables[:, 2 * L:4 * L].rearrange("p (n l) -> p n l", n=2)
        last = sb("last", [P, 2 * D])
        mask = last[:, 0:D]
        wo = last[:, D:2 * D]
        wqkv_hi = sb("wqkv_hi", [P, 3 * D], f32r)
        wqkv_lo = sb("wqkv_lo", [P, 3 * D], f32r)
        bk_rot = sb("bk_rot", [P, 2, HALVES, D])
        wf = sb("wf", [P, 3, HIDDEN], i32)
        wf_f = sb("wf_f", [P, 3, HIDDEN])
        wf_hi = sb("wf_hi", [P, 3, HIDDEN], f32r)
        wf_lo = sb("wf_lo", [P, 3, HIDDEN], f32r)
        largest = sb("largest", [P, 1])
        largest_all = sb("largest_all", [1, 1])
        warm = sb("warm", [P, N], mybir.dt.bfloat16)
        xs = sb("xs", [P, CHUNKS, TILES, D])
        oT = sb("oT", [P, 2, N])
        xn = sb("xn", [P, CHUNKS, TILES, D])
        outs = sb("outs", [P, CHUNKS, TILES * D])
        bn = sb("bn", [P, CHUNKS, TILES, 6])
        mv = sb("mv", [P, CHUNKS, TILES, 2])
        minus_half = sb("minus_half", [P, TILES])
        veps = sb("veps", [P, CHUNKS, TILES])
        rstd = sb("rstd", [P, CHUNKS, TILES])
        shift = sb("shift", [P, CHUNKS, TILES])
        xT_hi = sb("xT_hi", [P, 2, N], f32r)
        xT_lo = sb("xT_lo", [P, 2, N], f32r)
        q_cos = sb("q_cos", [P, 2, N])
        q_sin = sb("q_sin", [P, 2, N])
        k_cos = sb("k_cos", [P, 2, TILES, D])
        k_sin = sb("k_sin", [P, 2, TILES, D])
        k_rot = sb("k_rot", [P, 2, TILES, D])
        v = sb("v", [P, 2, TILES, D])
        kv = sb("kv", [P, BPC, D])
        kvo = sb("kvo", [P, BPC, D])
        kvo_swap = sb("kvo_swap", [P, BPC, D])
        silu = sb("silu", [P, 2, N])
        h = sb("h", [P, 2, N])
        h_hi = sb("h_hi", [P, 2, HB, N], f32r)
        h_lo = sb("h_lo", [P, 2, HB, N], f32r)

        p_gate = [pb("p_gate0"), pb("p_gate1")]
        p_up = [pb("p_up0"), pb("p_up1")]
        p_x = pb("p_x")
        p_kv = [pb("p_kv0"), pb("p_kv1")]
        p_out = pb("p_out")

        def q_bank(c):
            return p_out if c == 0 else p_x

        def sum_bank(c, b):
            return (p_kv[0], p_x)[b] if c == CHUNKS - 1 else p_out

        def back_bank(c, b):
            return (p_out, p_kv[1])[b] if c == CHUNKS - 1 else p_out

        def wait_h_lo(engine, c, j):
            if c < CHUNKS - 1:
                engine.wait_ge(h_lo_done, HB * c + j + 1)
            elif j == 1:
                engine.wait_ge(h_lo_done, HB * c + 1)
            else:
                engine.wait_ge(h_lo_by_vector, j // 2 + 1)

        x_in = [sem(f"x_in{c}") for c in range(CHUNKS)]
        first_in, wf_in, tables_in, last_in = (sem(n) for n in ("first_in", "wf_in", "tables_in", "last_in"))
        out_done = sem("out_done")
        consts_set = sem("consts_set")
        warm_set = sem("warm_set")
        table_loaded = sem("table_loaded")
        bk_parts_done = sem("bk_parts_done")
        bk_rot_done = sem("bk_rot_done")
        k_biased = sem("k_biased")
        wqkv_hi_done = sem("wqkv_hi_done")
        wqkv_lo_done = sem("wqkv_lo_done")
        wf_hi_done = sem("wf_hi_done")
        wf_f_done = sem("wf_f_done")
        wf_lo_done = sem("wf_lo_done")
        bn_done = sem("bn_done")
        mv_done = sem("mv_done")
        veps_done = sem("veps_done")
        rstd_done = sem("rstd_done")
        shift_done = sem("shift_done")
        xn_done = sem("xn_done")
        xn_first = sem("xn_first")
        largest_done = sem("largest_done")
        largest_turned = sem("largest_turned")
        largest_all_done = sem("largest_all_done")
        xT_made = sem("xT_made")
        xT_hi_done = sem("xT_hi_done")
        xT_lo_done = sem("xT_lo_done")
        q_made = sem("q_made")
        q_rotated = sem("q_rotated")
        kv_made = sem("kv_made")
        v_done = sem("v_done")
        k_sin_done = sem("k_sin_done")
        k_cos_done = sem("k_cos_done")
        k_rotated = sem("k_rotated")
        prod_made = sem("prod_made")
        prod_masked = sem("prod_masked")
        kvo_made = sem("kvo_made")
        kvo_done = sem("kvo_done")
        gu_made = sem("gu_made")
        silu_done = sem("silu_done")
        h_done = sem("h_done")
        h_hi_done = sem("h_hi_done")
        h_lo_done = sem("h_lo_done")
        h_lo_by_vector = sem("h_lo_by_vector")
        sum_made = sem("sum_made")
        sum_done = sem("sum_done")
        out_turned = sem("out_turned")
        out_added = sem("out_added")

        block = ctx.enter_context(nc.Block())

        x_view = x.rearrange("(c b) (p h) d -> c p b (h d)", b=BPC, h=HALVES)
        out_view = out.rearrange("(c b) (p h) d -> c p b (h d)", b=BPC, h=HALVES)

        @block.sync
        def _(sp):
            def load_x(c):
                sp.dma_start(xs[:, c].rearrange("p (b h) d -> p b (h d)", b=BPC), x_view[c]).then_inc(x_in[c], 16)

            load_x(0)
            sp.dma_start(first[:], early).then_inc(first_in, 16)
            load_x(1)
            sp.dma_start(wf[:], w_ffn).then_inc(wf_in, 16)
            sp.dma_start(tables[:], rope).then_inc(tables_in, 16)
            sp.dma_start(last[:], late).then_inc(last_in, 16)
            load_x(2)
            load_x(3)
            for c in range(CHUNKS):
                parts = BPC if c == CHUNKS - 1 else 1
                for s in range(parts):
                    sp.wait_ge(out_added, c + s + 1)
                    b = slice(s * BPC // parts, (s + 1) * BPC // parts)
                    sp.dma_start(out_view[c][:, b], outs[:, c].rearrange("p (b m) -> p b m", b=BPC)[:, b]
                                 ).then_inc(out_done, 16)
            sp.wait_ge(out_done, 16 * (CHUNKS - 1 + BPC))

        @block.gpsimd
        def _(pool):
            nc.gpsimd.memset(warm[:], 0.0).then_inc(warm_set, 1)
            nc.gpsimd.memset(minus_half[:], -0.5).then_inc(consts_set, 1)

            def inverse_spread(c):
                pool.wait_ge(veps_done, c + 1)
                if c == 0:
                    pool.wait_ge(consts_set, 1)
                nc.gpsimd.tensor_tensor(rstd[:, c], veps[:, c], minus_half[:], ALU.pow).then_inc(rstd_done, 1)

            def rotate_k(c, b):
                t = slice(HALVES * b, HALVES * (b + 1))
                pool.wait_ge(k_sin_done, 2 * (BPC * c + b + 1))
                nc.gpsimd.tensor_tensor(k_sin[:, c % 2, t], k_sin[:, c % 2, t], bk_rot[:, 0],
                                        ALU.add).then_inc(k_biased, 1)
                pool.wait_ge(k_biased, BPC * c + b + 1)
                pool.wait_ge(k_cos_done, BPC * c + b + 1)
                nc.gpsimd.tensor_tensor(k_rot[:, c % 2, t], k_cos[:, c % 2, t], k_sin[:, c % 2, t],
                                        ALU.add).then_inc(k_rotated, 1)

            def low_h(c, j):
                g = HB * c + j
                pool.wait_ge(h_hi_done, g + 1)
                nc.gpsimd.tensor_tensor(h_lo[:, c % 2, j], h[:, g % 2], h_hi[:, c % 2, j].bitcast(f32),
                                        ALU.subtract).then_inc(h_lo_done, 1)

            inverse_spread(0)
            inverse_spread(1)
            pool.wait_ge(tables_in, 16)
            bk = bkv[:, 0:D].rearrange("p (o d) -> p o d", o=1)
            nc.gpsimd.tensor_tensor(bk_rot[:, 0], bk.to_broadcast([P, HALVES, D]), rope_k[:, 0],
                                    ALU.mult).then_inc(bk_parts_done, 1)
            for s in range(2):
                nc.gpsimd.tensor_tensor(bk_rot[:, 1, :, s * SWAP:(s + 1) * SWAP],
                                        bk[:, :, (1 - s) * SWAP:(2 - s) * SWAP].to_broadcast([P, HALVES, SWAP]),
                                        rope_k[:, 1, :, s * SWAP:(s + 1) * SWAP], ALU.mult).then_inc(bk_parts_done, 1)
            pool.wait_ge(bk_parts_done, 3)
            nc.gpsimd.tensor_tensor(bk_rot[:, 0], bk_rot[:, 0], bk_rot[:, 1], ALU.add).then_inc(bk_rot_done, 1)
            pool.wait_ge(bk_rot_done, 1)
            rotate_k(0, 0)
            pool.wait_ge(largest_all_done, 1)
            bits = pool.value_load(largest_all[0:1, 0:1].bitcast(i32))
            with pool.If(bits > EXACT_BITS):
                pool.wait_ge(wf_hi_done, 1)
                nc.gpsimd.tensor_copy(wf_f[:], wf[:]).then_inc(wf_f_done, 1)
                pool.wait_ge(wf_f_done, 1)
                nc.gpsimd.tensor_tensor(wf_lo[:], wf_f[:], wf_hi[:].bitcast(f32),
                                        ALU.subtract).then_inc(wf_lo_done, 1)
            rotate_k(0, 1)
            for c in range(CHUNKS - 1):
                low_h(c, 0)
                if c == 1:
                    inverse_spread(3)
                low_h(c, 1)
                if c == 0:
                    inverse_spread(2)
                low_h(c, 2)
                rotate_k(c + 1, 0)
                rotate_k(c + 1, 1)
            low_h(CHUNKS - 1, 1)

        @block.scalar
        def _(act):
            act.wait_ge(warm_set, 1)
            nc.scalar.activation(silu[:, 0, 0:1], warm[:, 0:1], ACT.Silu).then_inc(table_loaded, 1)

            def normalise(c, tiles):
                act.wait_ge(shift_done, c + 1)
                for t in tiles:
                    nc.scalar.activation(xn[:, c, t], xs[:, c, t], ACT.Identity, bias=shift[:, c, t:t + 1],
                                         scale=rstd[:, c, t:t + 1]).then_inc(xn_done, 1)

            def high_xT(c):
                act.wait_ge(xT_made, TILES * (c + 1))
                nc.scalar.activation(xT_hi[:, c % 2], p_x[:], ACT.Copy).then_inc(xT_hi_done, 1)

            def gate(c, j):
                g = HB * c + j
                act.wait_ge(gu_made, g + 1)
                if g >= 2:
                    act.wait_ge(h_done, g - 1)
                nc.scalar.activation(silu[:, g % 2], p_gate[g % 2][:], ACT.Silu, scale=SCALE).then_inc(silu_done, 1)

            def high_h(c, j):
                g = HB * c + j
                act.wait_ge(h_done, g + 1)
                nc.scalar.activation(h_hi[:, c % 2, j], h[:, g % 2], ACT.Copy).then_inc(h_hi_done, 1)

            def products(c):
                act.wait_ge(kvo_made, c + 1)
                pv = p_kv[1][:, 0:BPC * D].rearrange("p (b d) -> p b d", b=BPC)
                nc.scalar.activation(kvo[:], pv, ACT.Copy).then_inc(kvo_done, 1)
                nc.scalar.activation(kvo_swap[0:SWAP], pv[SWAP:D], ACT.Copy).then_inc(kvo_done, 1)
                nc.scalar.activation(kvo_swap[SWAP:D], pv[0:SWAP], ACT.Copy).then_inc(kvo_done, 1)

            def summed(c, b, n):
                act.wait_ge(sum_made, (BPC * c + b + n))
                w = slice(b * L, (b + n) * L)
                nc.scalar.activation(oT[:, c % 2, w], sum_bank(c, b)[:, w], ACT.Identity,
                                     bias=bo).then_inc(sum_done, n)

            act.wait_ge(first_in, 16)
            nc.scalar.activation(wqkv_hi[:], wqkv, ACT.Copy).then_inc(wqkv_hi_done, 1)
            normalise(0, (2, 3))
            high_xT(0)
            act.wait_ge(wf_in, 16)
            nc.scalar.activation(wf_hi[:], wf[:], ACT.Copy).then_inc(wf_hi_done, 1)
            normalise(1, range(TILES))
            gate(0, 0)
            high_xT(1)
            gate(0, 1)
            high_h(0, 0)
            gate(0, 2)
            high_h(0, 1)
            high_h(0, 2)
            products(0)
            gate(1, 0)
            gate(1, 1)
            high_h(1, 0)
            normalise(2, range(TILES))
            for c in range(1, CHUNKS - 1):
                if c > 1:
                    gate(c, 0)
                    high_h(c, 0)
                    gate(c, 1)
                    high_h(c, 1)
                high_xT(c + 1)
                if c == 1:
                    high_h(1, 1)
                summed(c - 1, 0, BPC)
                gate(c, 2)
                products(c)
                high_h(c, 2)
                if c == 1:
                    normalise(3, range(TILES))
            c = CHUNKS - 1
            gate(c, 0)
            high_h(c, 0)
            gate(c, 1)
            gate(c, 2)
            high_h(c, 1)
            high_h(c, 2)
            summed(c - 1, 0, BPC)
            products(c)
            for b in range(BPC):
                summed(c, b, 1)

        @block.vector
        def _(dve):
            def statistics_of(c, tiles):
                dve.wait_ge(x_in[c], 16)
                for t in tiles:
                    nc.vector.bn_stats(bn[:, c, t], xs[:, c, t]).then_inc(bn_done, 1)

            def statistics(c, tiles=range(TILES)):
                statistics_of(c, tiles)
                for t in range(TILES):
                    dve.wait_ge(bn_done, TILES * c + t + 1)
                    nc.vector.bn_aggr(mv[:, c, t], bn[:, c, t]).then_inc(mv_done, 1)

            def spread(c):
                dve.wait_ge(mv_done, TILES * (c + 1))
                nc.vector.tensor_scalar(veps[:, c], mv[:, c, :, 1], EPS, None, ALU.add).then_inc(veps_done, 1)

            def shifts(c):
                dve.wait_ge(rstd_done, c + 1)
                nc.vector.scalar_tensor_tensor(out=shift[:, c], in0=mv[:, c, :, 0], scalar=-1.0, in1=rstd[:, c],
                                               op0=ALU.mult, op1=ALU.mult).then_inc(shift_done, 1)

            def low_xT(c):
                dve.wait_ge(xT_hi_done, c + 1)
                nc.vector.tensor_tensor(xT_lo[:, c % 2], p_x[:], xT_hi[:, c % 2].bitcast(f32),
                                        ALU.subtract).then_inc(xT_lo_done, 1)

            def rotate_q(c):
                dve.wait_ge(q_made, c + 1)
                q = q_bank(c)
                for n in range(2):
                    dst = (q_cos, q_sin)[n]
                    nc.vector.scalar_tensor_tensor(
                        out=dst[:, c % 2].rearrange("p (b l) -> p b l", b=BPC),
                        in0=q[:].rearrange("p (b l) -> p b l", b=BPC), scalar=bq,
                        in1=rope_q[:, n:n + 1, :].to_broadcast([P, BPC, L]),
                        op0=ALU.add, op1=ALU.mult).then_inc(q_rotated, 1)

            def keys_turned(c, b):
                dve.wait_ge(kv_made, HALVES * (BPC * c + b + 1))
                t = slice(HALVES * b, HALVES * (b + 1))
                k_v = p_kv[b][:].rearrange("p (t m) -> p t m", t=HALVES)
                for s in range(2):
                    nc.vector.tensor_tensor(k_sin[:, c % 2, t, s * SWAP:(s + 1) * SWAP],
                                            k_v[:, :, (1 - s) * SWAP:(2 - s) * SWAP],
                                            rope_k[:, 1, :, s * SWAP:(s + 1) * SWAP],
                                            ALU.mult).then_inc(k_sin_done, 1)

            def keys_straight(c, b):
                t = slice(HALVES * b, HALVES * (b + 1))
                k_v = p_kv[b][:].rearrange("p (t m) -> p t m", t=HALVES)
                nc.vector.tensor_tensor(k_cos[:, c % 2, t], k_v[:, :, 0:D], rope_k[:, 0], ALU.mult).then_inc(k_cos_done, 1)

            def values(c, b):
                t = slice(HALVES * b, HALVES * (b + 1))
                k_v = p_kv[b][:].rearrange("p (t m) -> p t m", t=HALVES)
                nc.vector.tensor_tensor(v[:, c % 2, t], k_v[:, :, D:2 * D],
                                        bkv[:, D:2 * D].rearrange("p (o d) -> p o d", o=1).to_broadcast([P, HALVES, D]),
                                        ALU.add).then_inc(v_done, 1)

            def hidden(c, j):
                g = HB * c + j
                dve.wait_ge(silu_done, g + 1)
                if g >= 2:
                    wait_h_lo(dve, *divmod(g - 2, HB))
                nc.vector.scalar_tensor_tensor(out=h[:, g % 2], in0=p_up[g % 2][:], scalar=SCALE * SCALE,
                                               in1=silu[:, g % 2], op0=ALU.mult, op1=ALU.mult).then_inc(h_done, 1)

            def low_h(c, j):
                g = HB * c + j
                dve.wait_ge(h_hi_done, g + 1)
                nc.vector.tensor_tensor(h_lo[:, c % 2, j], h[:, g % 2], h_hi[:, c % 2, j].bitcast(f32),
                                        ALU.subtract).then_inc(h_lo_by_vector, 1)

            def keep_heads(c):
                dve.wait_ge(prod_made, c + 1)
                nc.vector.tensor_tensor(kv[:], p_kv[0][:, 0:BPC * D].rearrange("p (b d) -> p b d", b=BPC),
                                        mask.rearrange("p (o d) -> p o d", o=1).to_broadcast([P, BPC, D]),
                                        ALU.mult).then_inc(prod_masked, 1)

            def finish(c, b, n):
                dve.wait_ge(out_turned, BPC * c + b + n)
                w = slice(b * L, (b + n) * L)
                nc.vector.tensor_tensor(outs[:, c, w], back_bank(c, b)[:, w],
                                        xs[:, c].rearrange("p t d -> p (t d)")[:, w], ALU.add).then_inc(out_added, 1)

            statistics(0)
            spread(0)
            dve.wait_ge(wqkv_hi_done, 1)
            nc.vector.tensor_tensor(wqkv_lo[:], wqkv, wqkv_hi[:].bitcast(f32),
                                    ALU.subtract).then_inc(wqkv_lo_done, 1)
            statistics_of(1, (0, 1))
            shifts(0)
            for t in (0, 1):
                nc.vector.tensor_scalar(xn[:, 0, t], xs[:, 0, t], mv[:, 0, t, 0:1], rstd[:, 0, t:t + 1],
                                        ALU.subtract, ALU.mult).then_inc(xn_first, 1)
            statistics(1, (2, 3))
            spread(1)
            dve.wait_ge(wf_in, 16)
            nc.vector.tensor_reduce(largest[:], wf[:], mybir.AxisListType.XY, ALU.max,
                                    apply_absolute_value=True).then_inc(largest_done, 1)
            low_xT(0)
            shifts(1)
            dve.wait_ge(largest_turned, 1)
            nc.vector.tensor_reduce(largest_all[:], p_up[1][0:1, 0:P], mybir.AxisListType.X,
                                    ALU.max).then_inc(largest_all_done, 1)
            dve.wait_ge(tables_in, 16)
            keys_turned(0, 0)
            keys_straight(0, 0)
            values(0, 0)
            keys_turned(0, 1)
            keys_straight(0, 1)
            hidden(0, 0)
            low_xT(1)
            values(0, 1)
            hidden(0, 1)
            statistics(2)
            spread(2)
            dve.wait_ge(last_in, 16)
            keep_heads(0)
            hidden(0, 2)
            rotate_q(0)
            shifts(2)
            keys_turned(1, 0)
            keys_straight(1, 0)
            values(1, 0)
            hidden(1, 0)
            keys_turned(1, 1)
            keys_straight(1, 1)
            rotate_q(1)
            values(1, 1)
            for c in range(1, CHUNKS - 1):
                hidden(c, 1)
                if c == 1:
                    statistics_of(3, range(TILES))
                keep_heads(c)
                low_xT(c + 1)
                if c == 1:
                    statistics(3, ())
                    spread(3)
                hidden(c, 2)
                if c == 1:
                    shifts(3)
                finish(c - 1, 0, BPC)
                rotate_q(c + 1)
                keys_turned(c + 1, 0)
                keys_straight(c + 1, 0)
                values(c + 1, 0)
                keys_turned(c + 1, 1)
                hidden(c + 1, 0)
                keys_straight(c + 1, 1)
                values(c + 1, 1)
            c = CHUNKS - 1
            low_h(c, 0)
            hidden(c, 1)
            keep_heads(c)
            hidden(c, 2)
            low_h(c, 2)
            finish(c - 1, 0, BPC)
            for b in range(BPC):
                finish(c, b, 1)

        @block.tensor
        def _(pe):
            def transpose_x(c):
                if c >= 2:
                    pe.wait_ge(q_rotated, 2 * c)
                for t in range(TILES):
                    if c == 0 and t < 2:
                        pe.wait_ge(xn_first, t + 1)
                    else:
                        pe.wait_ge(xn_done, TILES * c + t - 1)
                    nc.tensor.transpose(p_x[:, t * P:(t + 1) * P], xn[:, c, t], ident).then_inc(xT_made, 1)

            def project_first():
                xh, xl = xT_hi[:, 0], xT_lo[:, 0]

                def kv_passes(t, x_part, w_parts, start, stop):
                    b, half = divmod(t, HALVES)
                    for w in w_parts:
                        final = nc.tensor.matmul(p_kv[b][:, half * 2 * D:(half + 1) * 2 * D],
                                                 x_part[:, t * P:(t + 1) * P], w[:, D:3 * D],
                                                 start=start and w is w_parts[0], stop=stop)
                    return final

                pe.wait_ge(wqkv_lo_done, 1)
                pe.wait_ge(xT_hi_done, 1)
                for b in range(BPC):
                    kv_passes(HALVES * b, xh, (wqkv_hi, wqkv_lo), True, False)
                nc.tensor.matmul(p_out[:], wqkv_hi[:, 0:D], xh, start=True, stop=False)
                nc.tensor.matmul(p_out[:], wqkv_lo[:, 0:D], xh, start=False, stop=False)
                pe.wait_ge(largest_done, 1)
                nc.tensor.transpose(p_up[1][0:1, 0:P], largest[:], ident).then_inc(largest_turned, 1)
                pe.wait_ge(xT_lo_done, 1)
                for b in range(BPC):
                    t = HALVES * b
                    kv_passes(t, xl, (wqkv_hi,), False, True).then_inc(kv_made, 1)
                    for t in range(HALVES * b + 1, HALVES * (b + 1)):
                        kv_passes(t, xh, (wqkv_hi, wqkv_lo), True, False)
                        kv_passes(t, xl, (wqkv_hi,), False, True).then_inc(kv_made, 1)

            def project_q_last():
                nc.tensor.matmul(p_out[:], wqkv_hi[:, 0:D], xT_lo[:, 0], start=False, stop=True).then_inc(q_made, 1)

            def project_q(c):
                pe.wait_ge(xT_lo_done, c + 1)
                xh, xl = xT_hi[:, c % 2], xT_lo[:, c % 2]
                nc.tensor.matmul(p_x[:], wqkv_hi[:, 0:D], xh, start=True, stop=False)
                nc.tensor.matmul(p_x[:], wqkv_hi[:, 0:D], xl, start=False, stop=False)
                nc.tensor.matmul(p_x[:], wqkv_lo[:, 0:D], xh, start=False, stop=True).then_inc(q_made, 1)

            def project_kv(c, b):
                if b == 1 and c >= 1:
                    pe.wait_ge(kvo_done, 3 * c)
                for half in range(HALVES):
                    cols = slice((HALVES * b + half) * P, (HALVES * b + half + 1) * P)
                    dst = p_kv[b][:, half * 2 * D:(half + 1) * 2 * D]
                    xh, xl = xT_hi[:, c % 2, cols], xT_lo[:, c % 2, cols]
                    nc.tensor.matmul(dst, xh, wqkv_hi[:, D:3 * D], start=True, stop=False)
                    nc.tensor.matmul(dst, xh, wqkv_lo[:, D:3 * D], start=False, stop=False)
                    nc.tensor.matmul(dst, xl, wqkv_hi[:, D:3 * D], start=False, stop=True).then_inc(kv_made, 1)

            def gate_up(c, j, low):
                g = HB * c + j
                if g >= 2:
                    pe.wait_ge(silu_done, g - 1)
                    pe.wait_ge(h_done, g - 1)
                units = slice(j * P, (j + 1) * P)
                xh, xl = xT_hi[:, c % 2], xT_lo[:, c % 2]
                for m, bank in enumerate((p_gate[g % 2], p_up[g % 2])):
                    nc.tensor.matmul(bank[:], wf_hi[:, m, units], xh, start=True, stop=False)
                    if low:
                        nc.tensor.matmul(bank[:], wf_lo[:, m, units], xh, start=False, stop=False)
                    final = nc.tensor.matmul(bank[:], wf_hi[:, m, units], xl, start=False, stop=True)
                final.then_inc(gu_made, 1)

            def keys_values(c):
                pe.wait_ge(k_rotated, BPC * (c + 1))
                pe.wait_ge(v_done, BPC * (c + 1))
                for b in range(BPC):
                    for half in range(HALVES):
                        t = HALVES * b + half
                        final = nc.tensor.matmul(p_kv[0][:, b * D:(b + 1) * D], v[:, c % 2, t], k_rot[:, c % 2, t],
                                                start=(half == 0), stop=(half == HALVES - 1))
                final.then_inc(prod_made, 1)

            def times_wo(c):
                pe.wait_ge(prod_masked, c + 1)
                for b in range(BPC):
                    final = nc.tensor.matmul(p_kv[1][:, b * D:(b + 1) * D], kv[:, b], wo, start=True, stop=True)
                final.then_inc(kvo_made, 1)

            def attended(c, b, first):
                cols = slice(b * L, (b + 1) * L)
                dst = sum_bank(c, b)[:, cols]
                nc.tensor.matmul(dst, kvo[:, b], q_cos[:, c % 2, cols], start=first, stop=False)
                nc.tensor.matmul(dst, kvo_swap[:, b], q_sin[:, c % 2, cols], start=False, stop=False)

            def down(c, b, j, low, first=False):
                cols = slice(b * L, (b + 1) * L)
                dst = sum_bank(c, b)[:, cols]
                w_hi, w_lo = wf_hi[:, 2, j * D:(j + 1) * D], wf_lo[:, 2, j * D:(j + 1) * D]
                hh, hl = h_hi[:, c % 2, j, cols], h_lo[:, c % 2, j, cols]
                nc.tensor.matmul(dst, w_hi, hh, start=first, stop=False)
                if low:
                    nc.tensor.matmul(dst, w_lo, hh, start=False, stop=False)
                final = nc.tensor.matmul(dst, w_hi, hl, start=False, stop=(j == HB - 1))
                if j == HB - 1:
                    final.then_inc(sum_made, 1)

            def sums(c, b, low):
                if b == 0:
                    if c >= 1:
                        pe.wait_ge(out_added, c)
                    pe.wait_ge(kvo_done, 3 * (c + 1))
                    pe.wait_ge(q_rotated, 2 * (c + 1))
                attended(c, b, first=True)
                for j in range(HB):
                    if b == 0:
                        wait_h_lo(pe, c, j)
                    down(c, b, j, low)

            def sums_begun(c, low):
                pe.wait_ge(q_rotated, 2 * (c + 1))
                for j in range(HB - 1):
                    wait_h_lo(pe, c, j)
                    for b in range(BPC):
                        down(c, b, j, low, first=(j == 0))

            def sums_rest(c, low):
                pe.wait_ge(kvo_done, 3 * (c + 1))
                for b in range(BPC):
                    attended(c, b, first=False)
                    if b == 0:
                        wait_h_lo(pe, c, HB - 1)
                    down(c, b, HB - 1, low)

            def turn_back(c):
                if c == CHUNKS - 1:
                    pe.wait_ge(out_added, c)
                for b in range(BPC):
                    pe.wait_ge(sum_done, BPC * c + (b + 1 if c == CHUNKS - 1 else BPC))
                    for t in range(HALVES * b, HALVES * (b + 1)):
                        cols = slice(t * P, (t + 1) * P)
                        final = nc.tensor.transpose(back_bank(c, b)[:, cols], oT[:, c % 2, cols], ident)
                    final.then_inc(out_turned, 1)

            def warm_up(n):
                for _ in range(n):
                    nc.tensor.matmul(p_out[:], warm[:, 0:P], warm[:], start=True, stop=True)

            def chunks(low):
                if low:
                    pe.wait_ge(wf_lo_done, 1)
                gate_up(0, 0, low)
                transpose_x(1)
                gate_up(0, 1, low)
                project_q_last()
                gate_up(0, 2, low)
                project_q(1)
                keys_values(0)
                gate_up(1, 0, low)
                times_wo(0)
                project_kv(1, 0)
                gate_up(1, 1, low)
                project_kv(1, 1)
                for c in range(1, CHUNKS - 1):
                    if c > 1:
                        gate_up(c, 0, low)
                        gate_up(c, 1, low)
                    for b in range(BPC):
                        sums(c - 1, b, low)
                    transpose_x(c + 1)
                    keys_values(c)
                    gate_up(c, 2, low)
                    times_wo(c)
                    turn_back(c - 1)
                    project_q(c + 1)
                    project_kv(c + 1, 0)
                    project_kv(c + 1, 1)
                c = CHUNKS - 1
                gate_up(c, 0, low)
                gate_up(c, 1, low)
                sums(c - 1, 0, low)
                gate_up(c, 2, low)
                keys_values(c)
                sums(c - 1, 1, low)
                times_wo(c)
                sums_begun(c, low)
                turn_back(c - 1)
                sums_rest(c, low)
                turn_back(c)

            pe.wait_ge(warm_set, 1)
            warm_up(WARM_UP)
            pe.wait_ge(first_in, 16)
            transpose_x(0)
            warm_up(WARM_BETWEEN)
            project_first()
            pe.wait_ge(wf_hi_done, 1)
            pe.wait_ge(last_in, 16)
            pe.wait_ge(largest_all_done, 1)
            bits = pe.value_load(largest_all[0:1, 0:1].bitcast(i32))
            with pe.If(bits > EXACT_BITS):
                chunks(True)
            with pe.Else():
                chunks(False)


def kernel(L0_attn_x, L0_attn_Wq, L0_attn_bq, L0_attn_Wk, L0_attn_bk, L0_attn_Wv, L0_attn_bv, L0_attn_Wo,
           L0_attn_bo, L0_ffn_w_gate, L0_ffn_w_up, L0_ffn_w_down):
    import numpy as np
    import concourse.bacc as bacc
    from concourse.bass_utils import run_bass_kernel_spmd

    f = np.float32
    part, pair, head = np.meshgrid(np.arange(2), np.arange(PAIRS), np.arange(HEADS), indexing="ij")
    order = (head * HD + 2 * pair + part).ravel()
    part, pair, head = part.ravel(), pair.ravel(), head.ravel()
    freqs = (f(1.0) / np.power(f(10000.0), np.arange(0, HD, 2, dtype=f))).astype(f)
    angles = (np.arange(L, dtype=f)[:, None] * freqs[None, :]).astype(f)
    cos, sin = np.cos(angles)[:, pair].astype(f), np.sin(angles)[:, pair].astype(f)
    sign = np.where(part == 0, f(1), f(-1))
    tab_k = np.stack([cos.reshape(P, HALVES, D), (-sign * sin).reshape(P, HALVES, D)], 1)
    tile_order = np.arange(L).reshape(P, HALVES).T.ravel()
    tab_q = np.stack([cos[tile_order].T, (sign * sin)[tile_order].T], 1)
    head_mask = np.where(np.arange(D)[:, None] // HD == head[None, :], f(1.0 / np.sqrt(HD)), f(0)).astype(f)

    a = {k: np.asarray(t) for k, t in dict(
        x=L0_attn_x, wq=L0_attn_Wq, wk=L0_attn_Wk, wv=L0_attn_Wv, wo=L0_attn_Wo, bq=L0_attn_bq, bk=L0_attn_bk,
        bv=L0_attn_bv, bo=L0_attn_bo, wg=L0_ffn_w_gate, wu=L0_ffn_w_up, wd=L0_ffn_w_down).items()}
    bias_rows = np.tile(np.concatenate([a["bk"][order], a["bv"]]), (P, 1))
    arrays = {
        "x": a["x"],
        "early": np.concatenate([np.eye(P, dtype=f), a["wq"][:, order], a["wk"][:, order], a["wv"], bias_rows,
                                 a["bq"][order][:, None], a["bo"][:, None]], 1),
        "w_ffn": np.stack([a["wg"].T, a["wu"].T,
                           a["wd"].T.reshape(HB, P, D).transpose(1, 0, 2).reshape(P, HIDDEN)], 1),
        "rope": np.concatenate([tab_k.reshape(P, -1), tab_q.reshape(P, -1)], 1),
        "late": np.concatenate([head_mask, a["wo"]], 1),
    }
    arrays = {k: np.ascontiguousarray(t) for k, t in arrays.items()}
    nc = bacc.Bacc("TRN2", target_bir_lowering=False, num_devices=1)
    args = [nc.dram_tensor(k, t.shape, mybir.dt.from_np(t.dtype), kind="ExternalInput").ap() for k, t in arrays.items()]
    args.append(nc.dram_tensor("out", (B, L, D), mybir.dt.float32, kind="ExternalOutput").ap())
    build(nc, *args)
    r = run_bass_kernel_spmd(nc, [arrays], core_ids=[0])
    return r.results[0]["out"]
```
